# Optimizing a Trainium2 kernel written in Bass

```python
import numpy as np
import jax
import jax.numpy as jnp

def _softmax(x, axis=-1):
    return jax.nn.softmax(x, axis=axis)
def _gelu(x):
    return jax.nn.gelu(x, approximate=True)
def _silu(x):
    return jax.nn.silu(x)
def _sigmoid(x):
    return jax.nn.sigmoid(x)
def _layernorm(x, axis=-1, eps=1e-5):
    m = jnp.mean(x, axis=axis, keepdims=True)
    v = jnp.var(x, axis=axis, keepdims=True)
    return (x - m) / jnp.sqrt(v + eps)
def _scatter_add(tgt, idx, src, axis=0):
    return tgt.at[idx].add(src)
def _segment_sum(src, seg, n):
    return jax.ops.segment_sum(src, seg, n)

kernel_name = 'mk_adj_preln_d4_adj_256_60f615'

def setup_inputs(seed: int = 0):
    np.random.seed(seed)
    _w = jnp.asarray
    def _rec_inputs():
        import jax
        import jax.numpy as jnp
        _gk = jax.random.key(seed)
        x = -0.0005207 + 1.001 * jax.random.normal(jax.random.fold_in(_gk, 1), (3327, 256), jnp.float32)
        _w = (1.0 + jnp.arange(3327, dtype=jnp.float32)) ** -0.5
        _w = _w / _w.mean()
        _pij = jnp.clip(0.00240457 * _w[:, None] * _w[None, :], 0.0, 1.0)
        _a = jax.random.uniform(jax.random.fold_in(_gk, 2), (3327, 3327)) < _pij
        _a = jnp.logical_or(_a, jnp.eye(3327, dtype=bool))
        _af = _a.astype(jnp.float32)
        _af = _af * jax.random.uniform(jax.random.fold_in(_gk, 3), (3327, 3327), jnp.float32, 0.05, 1)
        adj = _af
        return x, adj
    x, adj = _rec_inputs()
    def _L0_gnn_setup():
        import jax, jax.numpy as jnp
        import numpy as np
        N, F, OUT = (8192, 256, 256)
        key = jax.random.key(seed)
        k1, k2, k3, k4 = jax.random.split(key, 4)
        features = jax.random.normal(k1, (N, F), dtype=jnp.float32)
        adj = jax.random.uniform(k2, (N, N), dtype=jnp.float32)
        gain = float(np.sqrt(2.0))
        b_n = gain * np.sqrt(6.0 / (F + F))
        neigh_W = jax.random.uniform(k3, (F, F), dtype=jnp.float32, minval=-b_n, maxval=b_n)
        b_l = gain * np.sqrt(6.0 / (2 * F + OUT))
        lin_W = jax.random.uniform(k4, (OUT, 2 * F), dtype=jnp.float32, minval=-b_l, maxval=b_l)
        return {'features': features, 'adj': adj, 'neigh_W': neigh_W, 'lin_W': lin_W}
    _L0_gnn_all = _L0_gnn_setup()
    _L0_gnn_in = {k: v for k, v in _L0_gnn_all.items() if k in ('neigh_W', 'lin_W', )}
    del _L0_gnn_all

    def _L1_gnn_setup():
        import jax, jax.numpy as jnp
        import numpy as np
        N = 6144
        HID = 256
        T = 700
        DENSITY = 0.05
        key = jax.random.key(seed)
        k1, k2, k3, k4, k5, k6 = jax.random.split(key, 6)
        h = jax.random.normal(k1, (N, HID), dtype=jnp.float32)
        a = jax.random.uniform(k2, (N, N), dtype=jnp.float32)
        mask = jax.random.uniform(k3, (N, N)) < DENSITY
        adj = jnp.where(mask, a, 0.0)
        simlar = jax.random.normal(k4, (N, N), dtype=jnp.float32)
        s = 1.0 / np.sqrt(HID)
        W_proj = jax.random.uniform(k5, (HID, HID), minval=-s, maxval=s, dtype=jnp.float32)
        b_proj = jnp.zeros((HID,), dtype=jnp.float32)
        W_gcn = jax.random.uniform(k6, (HID, HID), minval=-s, maxval=s, dtype=jnp.float32)
        b_gcn = jnp.zeros((HID,), dtype=jnp.float32)
        return {'h': h, 'adj': adj, 'simlar': simlar, 'W_proj': W_proj, 'b_proj': b_proj, 'W_gcn': W_gcn, 'b_gcn': b_gcn}
    _L1_gnn_all = _L1_gnn_setup()
    _L1_gnn_in = {k: v for k, v in _L1_gnn_all.items() if k in ('W_proj', 'b_proj', 'W_gcn', 'b_gcn', )}
    del _L1_gnn_all

    def _L2_gnn_setup():
        import jax, jax.numpy as jnp
        import numpy as np
        N = 20000
        D = 256
        F = 256
        K = F // 8
        key = jax.random.key(seed)
        k1, k2, k3, k4, k5 = jax.random.split(key, 5)
        h = jax.random.normal(k1, (N, D), dtype=jnp.float32)
        adj = jax.random.uniform(k2, (N, N), dtype=jnp.float32)
        W1 = jax.random.normal(k3, (D, K), dtype=jnp.float32) * 0.05
        W2 = jax.random.normal(k4, (K, D, F), dtype=jnp.float32) * 0.05
        b = jax.random.normal(k5, (K, F), dtype=jnp.float32) * 0.05
        return {'h': h, 'adj': adj, 'W1': W1, 'W2': W2, 'b': b}
    _L2_gnn_all = _L2_gnn_setup()
    _L2_gnn_in = {k: v for k, v in _L2_gnn_all.items() if k in ('W1', 'W2', 'b', )}
    del _L2_gnn_all

    def _L3_gnn_setup():
        import jax, jax.numpy as jnp
        import numpy as np
        N = 8192
        EMB = 256
        EDGE_P = 0.004
        LN_EPS = 1e-05

        def _layernorm(h, g, b):
            mu = jnp.mean(h, axis=-1, keepdims=True)
            var = jnp.mean(jnp.square(h - mu), axis=-1, keepdims=True)
            return (h - mu) * jax.lax.rsqrt(var + LN_EPS) * g + b
        key = jax.random.key(seed)
        ks = jax.random.split(key, 10)
        x = jax.random.normal(ks[0], (N, EMB), dtype=jnp.float32)
        adj = (jax.random.uniform(ks[1], (N, N)) < EDGE_P).astype(jnp.float32)
        adj = jnp.fill_diagonal(adj, 1.0, inplace=False)
        s = 1.0 / np.sqrt(EMB)
        W1 = jax.random.normal(ks[2], (EMB, EMB), dtype=jnp.float32) * s
        b1 = jax.random.normal(ks[3], (EMB,), dtype=jnp.float32) * s
        W2 = jax.random.normal(ks[4], (EMB, EMB), dtype=jnp.float32) * s
        b2 = jax.random.normal(ks[5], (EMB,), dtype=jnp.float32) * s
        W3 = jax.random.normal(ks[6], (EMB, EMB), dtype=jnp.float32) * s
        b3 = jax.random.normal(ks[7], (EMB,), dtype=jnp.float32) * s
        ones = jnp.ones((EMB,), jnp.float32)
        zeros = jnp.zeros((EMB,), jnp.float32)
        return {'x': x, 'adj': adj, 'W1': W1, 'b1': b1, 'W2': W2, 'b2': b2, 'W3': W3, 'b3': b3, 'g1': ones, 'be1': zeros, 'g2': ones, 'be2': zeros, 'g3': ones, 'be3': zeros}
    _L3_gnn_all = _L3_gnn_setup()
    _L3_gnn_in = {k: v for k, v in _L3_gnn_all.items() if k in ('W1', 'b1', 'W2', 'b2', 'W3', 'b3', 'g1', 'be1', 'g2', 'be2', 'g3', 'be3', )}
    del _L3_gnn_all

    return {
        "x": x,
        "adj": adj,
        "L0_gnn_neigh_W": _L0_gnn_in["neigh_W"],
        "L0_gnn_lin_W": _L0_gnn_in["lin_W"],
        "L1_gnn_W_proj": _L1_gnn_in["W_proj"],
        "L1_gnn_b_proj": _L1_gnn_in["b_proj"],
        "L1_gnn_W_gcn": _L1_gnn_in["W_gcn"],
        "L1_gnn_b_gcn": _L1_gnn_in["b_gcn"],
        "L2_gnn_W1": _L2_gnn_in["W1"],
        "L2_gnn_W2": _L2_gnn_in["W2"],
        "L2_gnn_b": _L2_gnn_in["b"],
        "L3_gnn_W1": _L3_gnn_in["W1"],
        "L3_gnn_b1": _L3_gnn_in["b1"],
        "L3_gnn_W2": _L3_gnn_in["W2"],
        "L3_gnn_b2": _L3_gnn_in["b2"],
        "L3_gnn_W3": _L3_gnn_in["W3"],
        "L3_gnn_b3": _L3_gnn_in["b3"],
        "L3_gnn_g1": _L3_gnn_in["g1"],
        "L3_gnn_be1": _L3_gnn_in["be1"],
        "L3_gnn_g2": _L3_gnn_in["g2"],
        "L3_gnn_be2": _L3_gnn_in["be2"],
        "L3_gnn_g3": _L3_gnn_in["g3"],
        "L3_gnn_be3": _L3_gnn_in["be3"],
    }

def reference(x, adj, L0_gnn_neigh_W, L0_gnn_lin_W, L1_gnn_W_proj, L1_gnn_b_proj, L1_gnn_W_gcn, L1_gnn_b_gcn, L2_gnn_W1, L2_gnn_W2, L2_gnn_b, L3_gnn_W1, L3_gnn_b1, L3_gnn_W2, L3_gnn_b2, L3_gnn_W3, L3_gnn_b3, L3_gnn_g1, L3_gnn_be1, L3_gnn_g2, L3_gnn_be2, L3_gnn_g3, L3_gnn_be3):
    import jax
    import jax.numpy as jnp
    def _L0_gnn_ref(features, adj, neigh_W, lin_W):
        import jax, jax.numpy as jnp
        import numpy as np
        N, F, OUT = (8192, 256, 256)
        h = features @ neigh_W.T
        deg = adj.sum(axis=1, keepdims=True) + 1.0
        h = adj @ h / deg
        z = jnp.concatenate([features, h], axis=-1) @ lin_W.T
        return z

    def _L1_gnn_ref(h, adj, simlar, W_proj, b_proj, W_gcn, b_gcn):
        import jax, jax.numpy as jnp
        import numpy as np
        N = 6144
        HID = 256
        T = 700
        DENSITY = 0.05
        sim = jnp.tanh(adj * simlar)
        filt = sim * (adj > 0).astype(sim.dtype)
        vals, idx = jax.lax.top_k(filt, T)
        nnz = jnp.sum(filt != 0, axis=1)
        keep = jnp.arange(T)[None, :] < nnz[:, None]
        rows = jnp.arange(filt.shape[0])[:, None]
        new_adj = jnp.zeros_like(filt).at[rows, idx].set(jnp.where(keep, vals, 0.0))
        h2 = jnp.tanh(h @ W_proj + b_proj)
        feat = jax.nn.relu(new_adj @ (h2 @ W_gcn) + b_gcn)
        return feat

    def _L2_gnn_ref(h, adj, W1, W2, b):
        import jax, jax.numpy as jnp
        import numpy as np
        N = 20000
        D = 256
        F = 256
        K = F // 8
        node = h @ W1
        hw = jnp.einsum('nc,kcf->nkf', h, W2)
        x = jnp.einsum('nk,nkf->nf', node, hw)
        x = adj @ x
        x = x + node @ b
        return jax.nn.relu(x)

    def _L3_gnn_ref(x, adj, W1, b1, W2, b2, W3, b3, g1, be1, g2, be2, g3, be3):
        import jax, jax.numpy as jnp
        import numpy as np
        N = 8192
        EMB = 256
        EDGE_P = 0.004
        LN_EPS = 1e-05

        def _layernorm(h, g, b):
            mu = jnp.mean(h, axis=-1, keepdims=True)
            var = jnp.mean(jnp.square(h - mu), axis=-1, keepdims=True)
            return (h - mu) * jax.lax.rsqrt(var + LN_EPS) * g + b
        dinv = jnp.sum(adj, axis=-1) ** (-0.5)
        A = adj * dinv[:, None] * dinv[None, :]
        h1 = x @ W1 + b1
        n1 = _layernorm(jax.nn.relu(A @ h1) + h1, g1, be1)
        h2 = n1 @ W2 + b2
        n2 = _layernorm(jax.nn.relu(A @ h2) + n1, g2, be2)
        h3 = n2 @ W3 + b3
        n3 = _layernorm(jax.nn.relu(A @ h3) + n2, g3, be3)
        return n3

    h = jnp.maximum(_layernorm(x, axis=-1), 0.0)
    x = x + _L0_gnn_ref(h, adj, L0_gnn_neigh_W, L0_gnn_lin_W)
    h = jnp.maximum(_layernorm(x, axis=-1), 0.0)
    x = x + _L1_gnn_ref(h, adj, adj, L1_gnn_W_proj, L1_gnn_b_proj, L1_gnn_W_gcn, L1_gnn_b_gcn)
    h = jnp.maximum(_layernorm(x, axis=-1), 0.0)
    x = x + _L2_gnn_ref(h, adj, L2_gnn_W1, L2_gnn_W2, L2_gnn_b)
    h = jnp.maximum(_layernorm(x, axis=-1), 0.0)
    x = x + _L3_gnn_ref(h, adj, L3_gnn_W1, L3_gnn_b1, L3_gnn_W2, L3_gnn_b2, L3_gnn_W3, L3_gnn_b3, L3_gnn_g1, L3_gnn_be1, L3_gnn_g2, L3_gnn_be2, L3_gnn_g3, L3_gnn_be3)
    return x


_drawn_inputs = setup_inputs


def setup_inputs(seed=0):
    import zlib

    import numpy as np

    out = dict(_drawn_inputs(seed))
    spreads = {'L1_gnn_b_proj': (0.0, 0.1),
     'L1_gnn_b_gcn': (0.0, 0.1),
     'L3_gnn_g1': (1.0, 0.2),
     'L3_gnn_be1': (0.0, 0.34),
     'L3_gnn_g2': (1.0, 0.2),
     'L3_gnn_be2': (0.0, 0.371),
     'L3_gnn_g3': (1.0, 0.2),
     'L3_gnn_be3': (0.0, 0.435)}
    factors = {'L3_gnn_b1': 3.032, 'L3_gnn_b2': 7.935, 'L3_gnn_b3': 7.334}
    for name, (base, spread) in spreads.items():
        noise = np.random.default_rng([zlib.crc32(name.encode()), seed]).standard_normal(out[name].shape)
        drawn = base * np.exp(spread * noise) if base else spread * noise
        out[name] = jnp.asarray(drawn.astype(out[name].dtype))
    for name, factor in factors.items():
        out[name] = (out[name] * factor).astype(out[name].dtype)
    return out
```

```python
from contextlib import ExitStack

import concourse.bass as bass
from concourse import mybir

F32 = mybir.dt.float32
F32R = mybir.dt.float32r
BF16 = mybir.dt.bfloat16
I32 = mybir.dt.int32
ALU = mybir.AluOpType
ACT = mybir.ActivationFunctionType
AX = mybir.AxisListType

P = 128
N = 3327
T = (N + P - 1) // P
NP = T * P
F = 256
C = F // P
HB = T // 2
K = 32
TOP = 700
NBITS = 31
ONE = 4
HC = 2 * F + ONE
EPS = 1e-5
LAYER0, LAYER1, LAYER2, LAYER3A, LAYER3B, LAYER3C = range(6)
PRIME = 2
RAW_PRIME = 4
EIN_PRIME = 2 * T


class Tile:

    def __init__(self, u, s):
        self.u, self.s = u, s
        self.t = 2 * u + s

    def next(self):
        return Tile(self.u, 1) if self.s == 0 else Tile(self.u + 1, 0)

    def prev(self):
        return Tile(self.u, 0) if self.s == 1 else Tile(self.u - 1, 1)

    def before(self, t):
        return not isinstance(self.t, int) or self.t < t


LAST = Tile(T // 2 - 1, 1)


def tiles(eng, step):
    step(Tile(0, 0))
    step(Tile(0, 1))
    with eng.Fori(1, T // 2 - 1) as u:
        step(Tile(u, 0))
        step(Tile(u, 1))
    step(Tile(T // 2 - 1, 0))
    step(LAST)


def beyond(value):
    return not isinstance(value, int) or value > 0


def column(buf, t):
    return buf[:, t:t + 1] if isinstance(t, int) else buf[:, bass.ds(t, 1)]


def build(nc, x, adjn, adjb, adjf, neigh_w, lin_wt, w_proj, b_proj, w_gcn, b_gcn, e_w1, e_w2, e_b, w1, b1, w2, b2, w3, b3,
          g1, be1, g2, be2, g3, be3, out):
    with ExitStack() as ctx:
        def sb(name, shape, dt=F32):
            return ctx.enter_context(nc.sbuf_tensor(name, shape, dt))

        def sem(name):
            return ctx.enter_context(nc.semaphore(name))

        base = -(-nc.sbuf_base // 32) * 32
        X = sb("X", [P, T, F])
        H = sb("H", [P, T, HC], F32R)
        h_at = base + T * F * 4
        hn_at = h_at + T * HC * 4
        r_at = hn_at + T * F * 4
        HN = sb("HN", [P, T, F])
        R = sb("R", [P, T, F])
        ring_at = r_at + T * F * 4
        half = HB * P
        RAW = sb("RAW", [P, 2, half])
        HI = sb("HI", [P, 2, half], F32R)
        LO = sb("LO", [P, 2, half], F32R)
        def at(name, shape, dt, offset):
            return nc.alloc_sbuf_tensor_at(name, shape, dt, offset=offset)

        NZ = at("NZ", [P, 2, half], BF16, r_at)
        RAWX = at("RAWX", [P, 2, half], F32, r_at + 4 * half)
        ACC = at("ACC", [P, T, F], F32, r_at)
        hi_at = ring_at + 8 * half
        EW = at("EW", [P, 2, C, 2 * F], F32, hi_at)
        EHI = at("EHI", [P, 2, C, 2 * F], F32R, hi_at + 16 * F * C)
        ELO = at("ELO", [P, 2, C, 2 * F], F32R, hi_at + 32 * F * C)
        FROW = at("FROW", [P, NP], F32, h_at)
        FVAL = at("FVAL", [P, NP], F32, h_at + 4 * NP)
        FTMP = at("FTMP", [P, NP], F32, h_at + 8 * NP)
        FKEEP = at("FKEEP", [P, NP], F32, h_at + 12 * NP)
        early_at = -(-nc.sbuf_base // 32) * 32
        W = sb("W", [P, C, 2 * F])
        H2 = sb("H2", [P, F])
        H2HI = sb("H2HI", [P, F], F32R)
        H2LO = sb("H2LO", [P, F], F32R)
        WLO = sb("WLO", [P, C, 2 * F], F32R)
        EN = sb("EN", [P, C, K])
        ENHI = sb("ENHI", [P, C, K], F32R)
        ENLO = sb("ENLO", [P, C, K], F32R)
        SPARE = sb("SPARE", [P, half - (C * 2 * F + 3 * C * K)])
        RAWY = at("RAWY", [P, half], F32, early_at)
        RAWZ = at("RAWZ", [P, half], F32, early_at + 4 * (C * 2 * F + 3 * F))
        WHI = sb("WHI", [P, C, 2 * F], F32R)
        WONE = sb("WONE", [P, C, F])
        WONE_CUT = (WHI[:, 0, :].rearrange("p (a f) -> p a f", a=C), WHI[:, 1, :].rearrange("p (a f) -> p a f", a=C))
        BIAS = sb("BIAS", [P, F])
        GAIN = sb("GAIN", [P, F])
        SHIFT = sb("SHIFT", [P, F])
        BPC = sb("BPC", [P, C])
        NB = sb("NB", [P, F])
        CROSS = sb("CROSS", [P, F])
        SUM = sb("SUM", [P, F])
        SUM2 = sb("SUM2", [P, F])
        CMAX = sb("CMAX", [P, 1])
        CALL = sb("CALL", [P, 1])
        FLAG = sb("FLAG", [P, 1], I32)
        BITS = sb("BITS", [P, NBITS], I32)
        VBITS = sb("VBITS", [P, 1], I32)
        CAND = sb("CAND", [P, 1], I32)
        TAKE = sb("TAKE", [P, 1], I32)
        FCNT = sb("FCNT", [P, 1])
        ROOM = sb("ROOM", [P, 1])
        Y = sb("Y", [P, F])
        ROW = sb("ROW", [P, F])
        HTHI = sb("HTHI", [P, F], F32R)
        HTLO = sb("HTLO", [P, F], F32R)
        NODE = sb("NODE", [P, T, K])
        NST = sb("NST", [P, P])
        NTT = sb("NTT", [P, P])
        IDN = sb("IDN", [P, P])
        ONEB = sb("ONEB", [P, 2], BF16)
        DEG = sb("DEG", [P, T])
        CNT = sb("CNT", [P, T])
        PAD = sb("PAD", [P, T])
        DINV = sb("DINV", [P, T])
        RDEG = sb("RDEG", [P, 1])
        HALF = sb("HALF", [P, T])
        MINUS = sb("MINUS", [P, 1])
        EPSC = sb("EPSC", [P, 1])
        IDLE = sb("IDLE", [P, 2])
        ST = sb("ST", [P, 6])
        ST0 = sb("ST0", [P, T, 6])
        MV = sb("MV", [P, 2])
        MV0 = sb("MV0", [P, T, 2])
        VE = sb("VE", [P, T])
        RSTD = sb("RSTD", [P, T])
        NMR = sb("NMR", [P, T])
        NM = sb("NM", [P, 1])

        bank = [ctx.enter_context(nc.psum_tensor(f"bank{i}", [P, 512], F32)) for i in range(8)]
        pacc = bank[0:2]
        pt = bank[2]
        pd = bank[3]
        pcnt = bank[4:6]
        pcross = bank[6:8]
        pnode = bank[4]
        pturn = bank[4:8]
        pein = bank[4:8]
        prow = [bank[2], bank[4]]
        pden = [bank[3], bank[5]]

        x_in = [sem("x_in0"), sem("x_in1")]
        const_in, w0_in, par_in = sem("const_in"), sem("w0_in"), sem("par_in")
        nb_set, pool_set, ones_set, ident_set = sem("nb_set"), sem("pool_set"), sem("ones_set"), sem("ident_set")
        wc_done, wc_kept, w_hi, w_lo = sem("wc_done"), sem("wc_kept"), sem("w_hi"), sem("w_lo")
        st0_done, mv0_done, ve0_done, rstd0_done, nmr0_done = (
            sem("st0_done"), sem("mv0_done"), sem("ve0_done"), sem("rstd0_done"), sem("nmr0_done"))
        row0_ready, rt0_done, hthi0, htlo0, dense0_done, h0_hi, h0_lo, x0_added = (
            sem("row0_ready"), sem("rt0_done"), sem("hthi0"), sem("htlo0"), sem("dense0_done"), sem("h0_hi"),
            sem("h0_lo"), sem("x0_added"))
        raw_in = [sem(f"raw_in{i}") for i in range(4)]
        hi_ready, lo_ready, hi_used, lo_used = sem("hi_ready"), sem("lo_ready"), sem("hi_used"), sem("lo_used")
        nz_ready, nz_used = sem("nz_ready"), sem("nz_used")
        sq_ready, th_ready = sem("sq_ready"), sem("th_ready")
        cross_ready, sum_ready, sum2_ready, y_ready = (
            sem("cross_ready"), sem("sum_ready"), sem("sum2_ready"), sem("y_ready"))
        deg_kept, deg1_kept, rdeg_kept, cnt_kept = sem("deg_kept"), sem("deg1_kept"), sem("rdeg_kept"), sem("cnt_kept")
        st_done, mv_done, ve_done, rstd_done, nm_done, nmr_done = (
            sem("st_done"), sem("mv_done"), sem("ve_done"), sem("rstd_done"), sem("nm_done"), sem("nmr_done"))
        z_ready, zg_ready = sem("z_ready"), sem("zg_ready")
        row_ready, row_kept = sem("row_ready"), sem("row_kept")
        rt_done, hthi_ready, htlo_ready = sem("rt_done"), sem("hthi_ready"), sem("htlo_ready")
        ht_kept, crossb_ready = sem("ht_kept"), sem("crossb_ready")
        cmax_done, call_done, flag_done, bits_set = sem("cmax_done"), sem("call_done"), sem("flag_done"), sem("bits_set")
        frow_in, fsq_done, fval_done, fbit_done, fkeep_done, fturned, fout_ready, fout_done = (
            sem("frow_in"), sem("fsq_done"), sem("fval_done"), sem("fbit_done"), sem("fkeep_done"), sem("fturned"),
            sem("fout_ready"), sem("fout_done"))
        proj_done, tanh_done, h2hi_ready, h2lo_ready = (
            sem("proj_done"), sem("tanh_done"), sem("h2hi_ready"), sem("h2lo_ready"))
        dense_done, dense_kept = sem("dense_done"), sem("dense_kept")
        nst_ready, nt_done, ntt_ready = sem("nst_ready"), sem("nt_done"), sem("ntt_ready")
        dinv_pad, dinv_done = sem("dinv_pad"), sem("dinv_done")
        split_hi, split_lo = sem("split_hi"), sem("split_lo")
        ew_in = [sem("ew_in0"), sem("ew_in1")]
        ehi_ready, elo_ready = sem("ehi_ready"), sem("elo_ready")
        acc_zero, ein_done, ein_added = sem("acc_zero"), sem("ein_done"), sem("ein_added")
        out_ready, out_done = sem("out_ready"), sem("out_done")

        block = ctx.enter_context(nc.Block())

        def past(p, phases):
            return T * len([q for q in phases if q < p])

        ALL = range(6)
        DENSE = (LAYER0, LAYER1, LAYER2, LAYER3A, LAYER3B)
        L3 = (LAYER3A, LAYER3B, LAYER3C)
        E_GROUPS = K // 2
        FBLOCKS = -(-T // 4)

        def raw_of(p, k, q):
            if k.s == 0:
                return RAW[:, q, :]
            return RAWX[:, q, :] if p <= LAYER1 else (RAWY, RAWZ)[q][:, :]

        def raw_landed(p, k):
            return 16 * (T // 2 * p + k.u + 1)

        def main_of(p, s):
            return pacc[s][:, 0:F]

        def cross_of(p, s):
            return pcross[s][:, 0:F] if p == LAYER0 else pacc[s][:, F:2 * F]

        def hi_of(j):
            return H[:, j, 0:F]

        def lo_of(j):
            return H[:, j, F + ONE:HC]

        def cuts_before(p):
            return 0 if p == LAYER1 else T * p

        def cut_source(p):
            return {LAYER1: HN, LAYER2: ACC, LAYER3A: R, LAYER3B: HN, LAYER3C: HN}[p]

        OVERLAP = (LAYER3A, LAYER3B, LAYER3C)

        def weight(w, k=None):
            return WONE[:, :, :] if k is None else W[:, :, k * F:(k + 1) * F], w.rearrange("(a p) f -> p a f", p=P)

        def spread(buf, v):
            return buf[:, :], v.rearrange("(a f) -> a f", a=1).to_broadcast([P, F])

        loads_of = {
            LAYER0: [weight(w_proj, 0), weight(w_gcn, 1)],
            LAYER1: [spread(BIAS, b_gcn)],
            LAYER2: [weight(w1), spread(BIAS, b1)],
            LAYER3A: [weight(w2), spread(BIAS, b2), spread(GAIN, g1), spread(SHIFT, be1)],
            LAYER3B: [weight(w3), spread(BIAS, b3), spread(GAIN, g2), spread(SHIFT, be2)],
            LAYER3C: [spread(GAIN, g3), spread(SHIFT, be3)],
        }

        def par_count(p):
            return 16 * sum(len(loads_of[q]) for q in range(p + 1))

        @block.sync
        def _(sp):
            def load(p, k, source):
                for q in range(2):
                    n = 2 * T * p + 2 * k.t + q
                    sp.wait_ge(lo_ready, n + 1)
                    sp.dma_start(raw_of(p, k, q), source[k.t, :, q * half:(q + 1) * half]).then_inc(
                        raw_in[2 * k.s + q], 16)

            def load_all(p, source, first=0):
                with sp.Fori(first, T // 2) as u:
                    load(p, Tile(u, 0), source)
                    load(p, Tile(u, 1), source)

            load(LAYER0, Tile(0, 0), adjb)
            xs = x.rearrange("p (t f) -> p t f", t=T)
            sp.dma_start(X[:, 0:HB, :], xs[:, 0:HB, :]).then_inc(x_in[0], 16)
            sp.dma_start(X[:, HB:T, :], xs[:, HB:T, :]).then_inc(x_in[1], 16)
            sp.dma_start(R[:, T - 4:T - 2, :], neigh_w.rearrange("(a p) f -> p a f", p=P)).then_inc(w0_in, 16)
            sp.dma_start(R[:, T - 2:T, :], lin_wt[F:2 * F, :].rearrange("(a p) f -> p a f", p=P)).then_inc(w0_in, 16)
            sp.dma_start(W[:, :, F:2 * F], lin_wt[0:F, :].rearrange("(a p) f -> p a f", p=P)).then_inc(w0_in, 16)
            sp.dma_start(EN[:, :, :], e_w1.rearrange("(a p) k -> p a k", p=P)).then_inc(const_in, 16)
            sp.dma_start(BPC[:, :], b_proj).then_inc(const_in, 16)
            sp.wait_ge(nb_set, 1)
            sp.dma_start(NB[0:K, :], e_b).then_inc(const_in, 16)
            load(LAYER0, Tile(0, 1), adjb)
            load_all(LAYER0, adjb, 1)

            sp.wait_ge(flag_done, 1)
            flag = sp.value_load(FLAG[0:1, 0:1], min_val=0, max_val=1)
            with sp.If(flag):
                with sp.Fori(0, T) as t:
                    sp.wait_ge(fout_done, 16 * (t + 1))
                    sp.dma_start(FROW[:, :], adjn[t]).then_inc(frow_in, 16)
                    sp.wait_ge(fout_ready, FBLOCKS * (t + 1))
                    sp.dma_start(adjf[t], FTMP[:, :]).then_inc(fout_done, 16)
                sp.wait_ge(fout_done, 16 * (T + 1))
                load_all(LAYER1, adjf)
            with sp.Else():
                load_all(LAYER1, adjb)

            sp.wait_ge(lo_used, PRIME + 2 * T * LAYER2)
            sp.dma_start(EW[:, 0, :, :], e_w2[0]).then_inc(ew_in[0], 16)
            sp.dma_start(EW[:, 1, :, :], e_w2[1]).then_inc(ew_in[1], 16)
            with sp.Fori(1, E_GROUPS // 2) as g:
                for s in range(2):
                    sp.wait_ge(elo_ready, 2 * g + s - 1)
                    sp.dma_start(EW[:, s, :, :], e_w2[2 * g + s]).then_inc(ew_in[s], 16)
            sp.wait_ge(dense_done, T * LAYER2)
            for p in (LAYER2, LAYER3A, LAYER3B, LAYER3C):
                load_all(p, adjb)

        @block.gpsimd
        def _(pool):
            nc.gpsimd.memset(NB[:, :], 0.0).then_inc(nb_set, 1)
            nc.gpsimd.memset(IDN[:, :], 0.0).then_inc(ident_set, 1)
            nc.gpsimd.memset(PAD[:, :], 0.0).then_inc(ident_set, 1)
            nc.gpsimd.memset(HALF[:, :], -0.5).then_inc(pool_set, 1)
            nc.gpsimd.memset(NST[:, :], 0.0).then_inc(pool_set, 1)
            nc.gpsimd.memset(MINUS[:, :], -1.0).then_inc(pool_set, 1)
            nc.gpsimd.memset(EPSC[:, :], EPS).then_inc(pool_set, 1)
            pool.wait_ge(ident_set, 2)
            nc.gpsimd.affine_select(out=IDN[:, :], in_=IDN[:, :], compare_op=ALU.not_equal, fill=1.0, base=0,
                                    pattern=[[-1, P]], channel_multiplier=1).then_inc(ident_set, 1)
            nc.gpsimd.affine_select(out=PAD[:, :], in_=PAD[:, :], compare_op=ALU.is_gt, fill=1.0, base=N,
                                    pattern=[[-P, T]], channel_multiplier=-1).then_inc(ident_set, 1)
            for b in range(NBITS):
                nc.gpsimd.memset(BITS[:, b:b + 1], 1 << (NBITS - 1 - b)).then_inc(bits_set, 1)
            pool.wait_ge(pool_set, 4)
            pool.wait_ge(mv0_done, T)
            nc.gpsimd.tensor_scalar(VE[:, :], MV0[:, :, 1], EPS, None, ALU.add).then_inc(ve0_done, 1)
            pool.wait_ge(ve0_done, 1)
            nc.gpsimd.tensor_tensor(RSTD[:, :], VE[:, :], HALF[:, :], ALU.pow).then_inc(rstd0_done, 1)
            pool.wait_ge(rstd0_done, 1)
            nc.gpsimd.tensor_tensor(NMR[:, :], MV0[:, :, 0], RSTD[:, :], ALU.mult).then_inc(nmr0_done, 1)
            pool.wait_ge(nmr0_done, 1)
            nc.gpsimd.tensor_scalar(NMR[:, :], NMR[:, :], -1.0, None, ALU.mult).then_inc(nmr0_done, 1)

            for p in ALL:
                if p == LAYER1:
                    pool.wait_ge(cmax_done, 1)
                    nc.gpsimd.partition_all_reduce(CALL[:, :], CMAX[:, :], P, bass.bass_isa.ReduceOp.max).then_inc(
                        call_done, 1)
                    pool.wait_ge(deg_kept, T)
                    pool.wait_ge(ident_set, 4)
                    nc.gpsimd.tensor_tensor(DEG[:, :], DEG[:, :], PAD[:, :], ALU.add).then_inc(dinv_pad, 1)
                    pool.wait_ge(dinv_pad, 1)
                    nc.gpsimd.tensor_tensor(DINV[:, :], DEG[:, :], HALF[:, :], ALU.pow).then_inc(dinv_done, 1)
                if p == LAYER2:
                    pool.wait_ge(lo_ready, RAW_PRIME + 2 * T * LAYER2)
                    nc.gpsimd.memset(ACC[:, :, :], 0.0).then_inc(acc_zero, 1)

                def norm(k):
                    n = T * p + k.t
                    if p == LAYER1:
                        pool.wait_ge(par_in, par_count(p))
                        pool.wait_ge(cross_ready, n + 1)
                        nc.gpsimd.tensor_tensor(CROSS[:, :], CROSS[:, :], BIAS[:, :], ALU.add).then_inc(crossb_ready, 1)
                    pool.wait_ge(mv_done, n + 1)
                    nc.gpsimd.tensor_tensor(VE[:, 0:1], MV[:, 1:2], EPSC[:, :], ALU.add).then_inc(ve_done, 1)
                    pool.wait_ge(ve_done, n + 1)
                    if beyond(n):
                        pool.wait_ge(row_ready, n)
                    nc.gpsimd.tensor_tensor(RSTD[:, 0:1], VE[:, 0:1], HALF[:, 0:1], ALU.pow).then_inc(rstd_done, 1)
                    pool.wait_ge(rstd_done, n + 1)
                    nc.gpsimd.tensor_tensor(NM[:, :], MV[:, 0:1], MINUS[:, :], ALU.mult).then_inc(nm_done, 1)
                    pool.wait_ge(nm_done, n + 1)
                    nc.gpsimd.tensor_tensor(NMR[:, 0:1], NM[:, :], RSTD[:, 0:1], ALU.mult).then_inc(nmr_done, 1)
                    if p == LAYER1:
                        pool.wait_ge(htlo_ready, n + 1)
                        nc.gpsimd.tensor_tensor(HN[:, k.t, :], HTHI[:, :].bitcast(F32), HTLO[:, :].bitcast(F32),
                                                ALU.add).then_inc(ht_kept, 1)
                tiles(pool, norm)

        @block.scalar
        def _(act):
            act.sem_inc(lo_ready, RAW_PRIME)
            act.sem_inc(hi_used, PRIME)
            act.sem_inc(lo_used, PRIME)
            act.sem_inc(nz_used, PRIME)
            act.sem_inc(fout_done, 16)
            act.sem_inc(ein_done, EIN_PRIME)
            act.sem_inc(ein_added, EIN_PRIME)

            def squashed(p, k, q):
                if p == LAYER1:
                    raw = raw_of(p, k, q)
                    act.wait_ge(sq_ready, 2 * k.t + q + 1)
                    nc.scalar.activation(raw, raw, ACT.Tanh).then_inc(th_ready, 1)

            def hi(p, k, q):
                n = 2 * T * p + 2 * k.t + q
                if p == LAYER1:
                    act.wait_ge(th_ready, 2 * k.t + q + 1)
                else:
                    act.wait_ge(raw_in[2 * k.s + q], raw_landed(p, k))
                act.wait_ge(hi_used, n + 1)
                act.wait_ge(lo_ready, n + 3)
                nc.scalar.activation(HI[:, q, :], raw_of(p, k, q), ACT.Copy).then_inc(hi_ready, 1)

            def cross(p, k):
                n = T * p + k.t
                act.wait_ge(lo_used, PRIME + 2 * (n + 1))
                if beyond(n):
                    act.wait_ge(sum_ready, n)
                nc.scalar.activation(CROSS[:, :], cross_of(p, k.s), ACT.Copy).then_inc(cross_ready, 1)

            def row(p, k):
                n = T * p + k.t
                if p < LAYER3A:
                    act.wait_ge(nmr_done, n + 1)
                    if beyond(n):
                        act.wait_ge(rt_done, n)
                    nc.scalar.activation(ROW[:, :], X[:, k.t, :], ACT.Relu, bias=NMR[:, 0:1],
                                         scale=RSTD[:, 0:1]).then_inc(row_ready, 1)
                elif p < LAYER3C:
                    act.wait_ge(row_ready, n + 1)
                    nc.scalar.activation(R[:, k.t, :], ROW[:, :], ACT.Copy).then_inc(row_kept, 1)

            def turned(p, k):
                n = T * p + k.t
                if p == LAYER3C:
                    return
                act.wait_ge(rt_done, n + 1)
                if beyond(n):
                    act.wait_ge(dense_done, n)
                if p == LAYER1 and beyond(k.t):
                    act.wait_ge(ht_kept, k.t)
                nc.scalar.activation(HTHI[:, :], pt[:, 0:F], ACT.Copy).then_inc(hthi_ready, 1)

            def dense_1(p, k):
                n = T * p + k.t
                if p == LAYER0:
                    act.wait_ge(proj_done, k.t + 1)
                    for a in range(C):
                        nc.scalar.activation(H2[:, a * P:(a + 1) * P], pd[:, a * P:(a + 1) * P], ACT.Tanh,
                                             bias=BPC[:, a:a + 1]).then_inc(tanh_done, 1)
                    act.wait_ge(tanh_done, 2 * k.t + 2)
                    if beyond(k.t):
                        act.wait_ge(dense_done, k.t)
                    nc.scalar.activation(H2HI[:, :], H2[:, :], ACT.Copy).then_inc(h2hi_ready, 1)
                if p == LAYER1:
                    act.wait_ge(dense_done, n + 1)
                    nc.scalar.activation(NODE[:, k.t, :], pd[:, 0:K], ACT.Copy).then_inc(dense_kept, 1)
                if p == LAYER3C:
                    act.wait_ge(out_ready, k.t + 1)
                    act.dma_start(out[k.t], X[:, k.t, :]).then_inc(out_done, 16)

            def dense_2(p, k):
                if p == LAYER0:
                    act.wait_ge(dense_done, k.t + 1)
                    nc.scalar.activation(HN[:, k.t, :], pd[:, F:2 * F], ACT.Copy).then_inc(dense_kept, 1)

            def cut_h(p, j):
                act.wait_ge(lo_used, PRIME + 2 * T * p - (j < HB))
                src = cut_source(p)
                if p == LAYER2:
                    act.wait_ge(ein_added, EIN_PRIME + 2 * T * (E_GROUPS - 1) + min(2 * j + 3, 2 * T))
                    act.wait_ge(ein_done, EIN_PRIME + T * E_GROUPS)
                else:
                    act.wait_ge(dense_kept, T * (p - 1) + j + 1)
                if p in L3:
                    nc.scalar.activation(hi_of(j), src[:, j, :], ACT.Copy, scale=DINV[:, j:j + 1]).then_inc(split_hi, 1)
                else:
                    nc.scalar.activation(hi_of(j), src[:, j, :], ACT.Copy).then_inc(split_hi, 1)

            def params(p):
                if p == LAYER0:
                    act.wait_ge(dense0_done, T)
                    act.wait_ge(w_lo, 2)
                else:
                    act.wait_ge(row_ready, T * p)
                    act.wait_ge(dense_done, past(p, DENSE))
                    act.wait_ge(dense_kept, past(p, DENSE))
                for dst, src in loads_of[p]:
                    act.dma_start(dst, src).then_inc(par_in, 16)

            def weights_hi(p):
                if p not in (LAYER1, LAYER3C):
                    act.wait_ge(par_in, par_count(p))
                    whole, high = (W, WHI) if p == LAYER0 else (WONE, WONE_CUT[0])
                    nc.scalar.activation(high[:, :, :], whole[:, :, :], ACT.Copy).then_inc(w_hi, 1)

            first = Tile(0, 0)
            hi(LAYER0, first, 0)
            hi(LAYER0, first, 1)

            act.wait_ge(wc_done, 1)
            act.wait_ge(w0_in, 48)
            nc.scalar.activation(W[:, :, 0:F], pd[:, :].rearrange("p (a f) -> p a f", a=C), ACT.Copy).then_inc(wc_kept, 1)
            act.wait_ge(wc_kept, 1)
            nc.scalar.activation(WHI[:, :, :], W[:, :, :], ACT.Copy).then_inc(w_hi, 1)
            act.wait_ge(const_in, 48)
            nc.scalar.activation(ENHI[:, :, :], EN[:, :, :], ACT.Copy).then_inc(w_hi, 1)
            act.wait_ge(nmr0_done, 2)
            rows, hthi = [ROW, Y], [HTHI, H2HI]

            def row0(k):
                if beyond(k.t - 1):
                    act.wait_ge(rt0_done, k.t - 1)
                nc.scalar.activation(rows[k.s][:, :], X[:, k.t, :], ACT.Relu, bias=column(NMR, k.t),
                                     scale=column(RSTD, k.t)).then_inc(row0_ready, 1)

            def step0(k):
                if k.before(T - 1):
                    row0(k.next())
                act.wait_ge(rt0_done, k.t + 1)
                if beyond(k.t - 1):
                    act.wait_ge(dense0_done, k.t - 1)
                nc.scalar.activation(hthi[k.s][:, :], prow[k.s][:, 0:F], ACT.Copy).then_inc(hthi0, 1)
                if beyond(k.t):
                    keep0(k.prev())

            def keep0(k):
                act.wait_ge(dense0_done, k.t + 1)
                nc.scalar.activation(hi_of(k.t), pden[k.s][:, 0:F], ACT.Copy).then_inc(h0_hi, 1)
            row0(first)
            tiles(act, step0)
            keep0(LAST)
            params(LAYER0)
            weights_hi(LAYER0)

            for p in ALL:
                if p == LAYER1:
                    act.wait_ge(flag_done, 1)
                    flag = act.value_load(FLAG[0:1, 0:1], min_val=0, max_val=1)
                    with act.If(flag):
                        with act.Fori(0, T) as t:
                            act.wait_ge(fsq_done, t + 1)
                            nc.scalar.activation(FVAL[:, :], FTMP[:, :], ACT.Tanh).then_inc(fval_done, 1)
                            for b in range(FBLOCKS):
                                w = min(4 * P, NP - 4 * P * b)
                                act.wait_ge(fturned, FBLOCKS * t + b + 1)
                                nc.scalar.activation(FTMP[:, 4 * P * b:4 * P * b + w], pturn[b % 4][:, 0:w],
                                                     ACT.Copy).then_inc(fout_ready, 1)
                    act.wait_ge(flag_done, 1)
                if p == LAYER2:
                    act.wait_ge(ht_kept, T)
                    act.wait_ge(lo_used, PRIME + 2 * T * p)

                    def cut_e(g, s):
                        act.wait_ge(ew_in[s], 16 * (g + 1))
                        act.wait_ge(ein_done, T * (2 * g + s + 1))
                        nc.scalar.activation(EHI[:, s, :, :], EW[:, s, :, :], ACT.Copy).then_inc(ehi_ready, 1)
                    cut_e(0, 0)
                    for j in range(T):
                        nc.scalar.activation(hi_of(j), HN[:, j, :], ACT.Copy).then_inc(split_hi, 1)
                    cut_e(0, 1)
                    with act.Fori(1, E_GROUPS // 2) as g:
                        cut_e(g, 0)
                        cut_e(g, 1)
                    act.wait_ge(ein_done, EIN_PRIME + T * E_GROUPS)
                if p in (LAYER1, LAYER2):
                    squashed(p, first, 0)
                    hi(p, first, 0)
                    for j in range(HB):
                        cut_h(p, j)
                    squashed(p, first, 1)
                    hi(p, first, 1)
                    for j in range(HB, T):
                        cut_h(p, j)
                    weights_hi(p)

                def step(k):
                    if p == LAYER2:
                        act.wait_ge(nt_done, k.t + 1)
                        nc.scalar.activation(NTT[:, :], pnode[:, 0:P], ACT.Copy).then_inc(ntt_ready, 1)
                    old = beyond(k.t)
                    new = k.before(T - 1)
                    if old:
                        cross(p, k.prev())
                    if new:
                        squashed(p, k.next(), 0)
                        hi(p, k.next(), 0)
                    if beyond(k.t - 1):
                        dense_2(p, k.prev().prev())
                    if old:
                        row(p, k.prev())
                    if new:
                        squashed(p, k.next(), 1)
                    if old:
                        turned(p, k.prev())
                    if new:
                        hi(p, k.next(), 1)
                    if old:
                        dense_1(p, k.prev())
                tiles(act, step)
                after = p + 1 if p + 1 in OVERLAP else None
                if after:
                    for j in range(HB):
                        cut_h(after, j)
                cross(p, LAST)
                if after:
                    hi(after, first, 0)
                dense_2(p, LAST.prev())
                row(p, LAST)
                if after:
                    hi(after, first, 1)
                turned(p, LAST)
                dense_1(p, LAST)
                dense_2(p, LAST)
                if after:
                    for j in range(HB, T):
                        cut_h(after, j)
                if p != LAYER3C:
                    params(p + 1)
                if after:
                    weights_hi(after)
            act.wait_ge(out_done, 16 * T)

        @block.vector
        def _(dve):
            nc.vector.memset(H[:, :, F:F + ONE].bitcast(F32), 1.0).then_inc(ones_set, 1)
            nc.vector.memset(ONEB[:, :], 1.0).then_inc(ones_set, 1)

            def positive(p, k, q):
                if p == LAYER0:
                    n = 2 * k.t + q
                    dve.wait_ge(raw_in[2 * k.s + q], raw_landed(p, k))
                    dve.wait_ge(nz_used, n + 1)
                    nc.vector.tensor_scalar(NZ[:, q, :], raw_of(p, k, q), 0.0, None, ALU.is_gt).then_inc(nz_ready, 1)

            def squared(p, k, q):
                if p == LAYER1:
                    raw = raw_of(p, k, q)
                    dve.wait_ge(raw_in[2 * k.s + q], raw_landed(p, k))
                    nc.vector.scalar_tensor_tensor(out=raw, in0=raw, scalar=0.0, in1=raw, op0=ALU.max,
                                                   op1=ALU.mult).then_inc(sq_ready, 1)

            def lo(p, k, q):
                n = 2 * T * p + 2 * k.t + q
                dve.wait_ge(hi_ready, n + 1)
                dve.wait_ge(lo_used, n + 1)
                nc.vector.tensor_tensor(LO[:, q, :], raw_of(p, k, q), HI[:, q, :].bitcast(F32),
                                        ALU.subtract).then_inc(lo_ready, 1)

            def sums(p, k):
                n, t = T * p + k.t, k.t
                if p == LAYER0:
                    deg = pacc[k.s][:, F:F + 1]
                    dve.wait_ge(lo_used, PRIME + 2 * (n + 1))
                    nc.vector.tensor_copy(column(DEG, t), deg).then_inc(deg_kept, 1)
                    nc.vector.tensor_scalar(RDEG[:, :], deg, 1.0, None, ALU.add).then_inc(deg1_kept, 1)
                    dve.wait_ge(deg1_kept, t + 1)
                    nc.vector.reciprocal(RDEG[:, :], RDEG[:, :]).then_inc(rdeg_kept, 1)
                    dve.wait_ge(nz_used, PRIME + 2 * (n + 1))
                    nc.vector.tensor_copy(column(CNT, t), pcnt[k.s][:, 0:1]).then_inc(cnt_kept, 1)
                if p == LAYER1:
                    dve.wait_ge(crossb_ready, t + 1)
                dve.wait_ge(cross_ready, n + 1)
                nc.vector.tensor_tensor(SUM[:, :], main_of(p, k.s), CROSS[:, :], ALU.add).then_inc(sum_ready, 1)
                dve.wait_ge(sum_ready, n + 1)
                if p == LAYER0:
                    dve.wait_ge(rdeg_kept, t + 1)
                    nc.vector.scalar_tensor_tensor(out=X[:, t, :], in0=SUM[:, :], scalar=RDEG[:, 0:1],
                                                   in1=X[:, t, :], op0=ALU.mult, op1=ALU.add).then_inc(y_ready, 1)
                elif p in (LAYER1, LAYER2):
                    nc.vector.scalar_tensor_tensor(out=X[:, t, :], in0=SUM[:, :], scalar=0.0, in1=X[:, t, :],
                                                   op0=ALU.max, op1=ALU.add).then_inc(y_ready, 1)
                else:
                    nc.vector.tensor_scalar(SUM2[:, :], SUM[:, :], 0.0, column(DINV, t), ALU.max,
                                            ALU.mult).then_inc(sum2_ready, 1)
                    dve.wait_ge(sum2_ready, past(p, L3) + t + 1)
                    nc.vector.tensor_tensor(Y[:, :], SUM2[:, :], R[:, t, :], ALU.add).then_inc(y_ready, 1)
                dve.wait_ge(y_ready, n + 1)
                nc.vector.memset(IDLE[:, 0:1], 0.0)
                nc.vector.bn_stats(ST[:, :], Y[:, :] if p in L3 else X[:, t, :]).then_inc(st_done, 1)
                if beyond(n):
                    dve.wait_ge(nmr_done, n)
                dve.wait_ge(st_done, n + 1)
                nc.vector.memset(IDLE[:, 1:2], 0.0)
                nc.vector.bn_aggr(MV[:, :], ST[:, :]).then_inc(mv_done, 1)

            def scaled(p, k):
                n = T * p + k.t
                m = past(p, L3) + k.t
                if p not in L3:
                    return
                dve.wait_ge(rstd_done, n + 1)
                nc.vector.tensor_scalar(SUM2[:, :], Y[:, :], MV[:, 0:1], RSTD[:, 0:1], ALU.subtract,
                                        ALU.mult).then_inc(z_ready, 1)
                dve.wait_ge(z_ready, m + 1)
                nc.vector.tensor_tensor(SUM2[:, :], SUM2[:, :], GAIN[:, :], ALU.mult).then_inc(zg_ready, 1)
                dve.wait_ge(zg_ready, m + 1)
                if p != LAYER3C:
                    dve.wait_ge(rt_done, n)
                    if beyond(m):
                        dve.wait_ge(row_kept, m)
                    nc.vector.tensor_tensor(ROW[:, :], SUM2[:, :], SHIFT[:, :], ALU.add).then_inc(row_ready, 1)
                else:
                    nc.vector.tensor_tensor(SUM2[:, :], SUM2[:, :], SHIFT[:, :], ALU.add).then_inc(row_ready, 1)
                    dve.wait_ge(row_ready, n + 1)
                    nc.vector.tensor_tensor(X[:, k.t, :], SUM2[:, :], X[:, k.t, :], ALU.add).then_inc(out_ready, 1)

            def turned(p, k):
                if p == LAYER3C:
                    return
                dve.wait_ge(hthi_ready, T * p + k.t + 1)
                nc.vector.tensor_tensor(HTLO[:, :], pt[:, 0:F], HTHI[:, :].bitcast(F32), ALU.subtract).then_inc(
                    htlo_ready, 1)

            def dense(p, k):
                if p == LAYER0:
                    dve.wait_ge(h2hi_ready, k.t + 1)
                    nc.vector.tensor_tensor(H2LO[:, :], H2[:, :], H2HI[:, :].bitcast(F32), ALU.subtract).then_inc(
                        h2lo_ready, 1)
                if p in (LAYER2, LAYER3A, LAYER3B):
                    dve.wait_ge(dense_done, T * p + k.t + 1)
                    nc.vector.tensor_tensor((R if p == LAYER2 else HN)[:, k.t, :], pd[:, 0:F], BIAS[:, :],
                                            ALU.add).then_inc(dense_kept, 1)

            def node(p, k):
                if p == LAYER2:
                    if beyond(k.t):
                        dve.wait_ge(nt_done, k.t)
                    nc.vector.tensor_copy(NST[:, 0:K], NODE[:, k.t, :]).then_inc(nst_ready, 1)

            def cut_h(p, j):
                src = cut_source(p)
                dve.wait_ge(split_hi, cuts_before(p) + j + 1)
                if p in L3:
                    nc.vector.scalar_tensor_tensor(out=lo_of(j), in0=src[:, j, :], scalar=DINV[:, j:j + 1],
                                                   in1=hi_of(j).bitcast(F32), op0=ALU.mult,
                                                   op1=ALU.subtract).then_inc(split_lo, 1)
                else:
                    nc.vector.tensor_tensor(lo_of(j), src[:, j, :], hi_of(j).bitcast(F32), ALU.subtract).then_inc(
                        split_lo, 1)

            cuts = [2]

            def weights_lo(p):
                if p in (LAYER0, LAYER2, LAYER3A, LAYER3B):
                    cuts[0] += 1
                    dve.wait_ge(w_hi, cuts[0])
                    whole, high, low = (W, WHI[:, :, :], WLO) if p == LAYER0 else (WONE, *WONE_CUT)
                    nc.vector.tensor_tensor(low[:, :, :], whole[:, :, :], high.bitcast(F32), ALU.subtract).then_inc(w_lo, 1)
                dve.wait_ge(par_in, par_count(p))

            first = Tile(0, 0)
            positive(LAYER0, first, 0)
            lo(LAYER0, first, 0)
            positive(LAYER0, first, 1)
            lo(LAYER0, first, 1)
            for t in range(T):
                if t in (0, HB):
                    dve.wait_ge(x_in[t // HB], 16)
                nc.vector.bn_stats(ST0[:, t, :], X[:, t, :]).then_inc(st0_done, 1)
            for t in range(T):
                dve.wait_ge(st0_done, t + 1)
                nc.vector.bn_aggr(MV0[:, t, :], ST0[:, t, :]).then_inc(mv0_done, 1)
            dve.wait_ge(w_hi, 1)
            nc.vector.tensor_tensor(WLO[:, :, :], W[:, :, :], WHI[:, :, :].bitcast(F32), ALU.subtract).then_inc(w_lo, 1)
            dve.wait_ge(w_hi, 2)
            nc.vector.tensor_tensor(ENLO[:, :, :], EN[:, :, :], ENHI[:, :, :].bitcast(F32), ALU.subtract).then_inc(w_lo, 1)
            hthi, htlo = [HTHI, H2HI], [HTLO, H2LO]

            def step0(k):
                dve.wait_ge(hthi0, k.t + 1)
                if beyond(k.t - 1):
                    dve.wait_ge(dense0_done, k.t - 1)
                nc.vector.tensor_tensor(htlo[k.s][:, :], prow[k.s][:, 0:F], hthi[k.s][:, :].bitcast(F32),
                                        ALU.subtract).then_inc(htlo0, 1)
                if beyond(k.t):
                    keep0(k.prev())

            def keep0(k):
                dve.wait_ge(h0_hi, k.t + 1)
                nc.vector.tensor_tensor(lo_of(k.t), pden[k.s][:, 0:F], hi_of(k.t).bitcast(F32), ALU.subtract).then_inc(
                    h0_lo, 1)
                dve.wait_ge(row0_ready, k.t + 1)
                nc.vector.tensor_tensor(X[:, k.t, :], pden[k.s][:, F:2 * F], X[:, k.t, :], ALU.add).then_inc(x0_added, 1)
            tiles(dve, step0)
            keep0(LAST)
            weights_lo(LAYER0)

            for p in ALL:
                if p == LAYER1:
                    dve.wait_ge(cnt_kept, T)
                    nc.vector.tensor_reduce(CMAX[:, :], CNT[:, :], AX.X, ALU.max).then_inc(cmax_done, 1)
                    dve.wait_ge(call_done, 1)
                    nc.vector.tensor_scalar(FLAG[:, :], CALL[:, :], float(TOP), None, ALU.is_gt).then_inc(flag_done, 1)
                    dve.wait_ge(flag_done, 1)
                    flag = dve.value_load(FLAG[0:1, 0:1], min_val=0, max_val=1)
                    with dve.If(flag):
                        dve.wait_ge(bits_set, NBITS)
                        with dve.Fori(0, T) as t:
                            dve.wait_ge(frow_in, 16 * (t + 1))
                            nc.vector.scalar_tensor_tensor(out=FTMP[:, :], in0=FROW[:, :], scalar=0.0, in1=FROW[:, :],
                                                           op0=ALU.max, op1=ALU.mult).then_inc(fsq_done, 1)
                            per = 4 * NBITS + 7
                            dve.wait_ge(fval_done, t + 1)
                            nc.vector.memset(VBITS[:, :], 0).then_inc(fbit_done, 1)
                            with dve.Fori(0, NBITS) as b:
                                done = per * t + 1 + 4 * b
                                dve.wait_ge(fbit_done, done)
                                nc.vector.tensor_tensor(CAND[:, :], VBITS[:, :], BITS[:, bass.ds(b, 1)],
                                                        ALU.bitwise_or).then_inc(fbit_done, 1)
                                dve.wait_ge(fbit_done, done + 1)
                                nc.vector.tensor_scalar(FTMP[:, :], FVAL[:, :], CAND[:, :].bitcast(F32), 0.0, ALU.is_ge,
                                                        ALU.add, accum_out=FCNT[:, :]).then_inc(fbit_done, 1)
                                dve.wait_ge(fbit_done, done + 2)
                                nc.vector.tensor_scalar(TAKE[:, :], FCNT[:, :], float(TOP), None,
                                                        ALU.is_ge).then_inc(fbit_done, 1)
                                dve.wait_ge(fbit_done, done + 3)
                                nc.vector.memset(IDLE[:, 0:1], 0.0)
                                nc.vector.copy_predicated(VBITS[:, :], TAKE[:, :], CAND[:, :]).then_inc(fbit_done, 1)
                            least = VBITS[:, :].bitcast(F32)
                            done = per * t + 1 + 4 * NBITS
                            dve.wait_ge(fbit_done, done)
                            nc.vector.tensor_scalar(FTMP[:, :], FVAL[:, :], least, 0.0, ALU.is_gt, ALU.add,
                                                    accum_out=FCNT[:, :]).then_inc(fbit_done, 1)
                            dve.wait_ge(fbit_done, done + 1)
                            nc.vector.tensor_scalar(ROOM[:, :], FCNT[:, :], -1.0, float(TOP), ALU.mult,
                                                    ALU.add).then_inc(fbit_done, 1)
                            dve.wait_ge(fbit_done, done + 2)
                            nc.vector.tensor_scalar(FTMP[:, :], FVAL[:, :], least, None, ALU.is_equal).then_inc(
                                fbit_done, 1)
                            dve.wait_ge(fbit_done, done + 3)
                            nc.vector.tensor_tensor_scan(FKEEP[:, :], FTMP[:, :], FTMP[:, :], 0.0, ALU.add,
                                                         ALU.max).then_inc(fbit_done, 1)
                            dve.wait_ge(fbit_done, done + 4)
                            nc.vector.scalar_tensor_tensor(out=FKEEP[:, :], in0=FKEEP[:, :], scalar=ROOM[:, :],
                                                           in1=FTMP[:, :], op0=ALU.is_le, op1=ALU.mult).then_inc(
                                fbit_done, 1)
                            dve.wait_ge(fbit_done, done + 5)
                            nc.vector.scalar_tensor_tensor(out=FKEEP[:, :], in0=FVAL[:, :], scalar=least,
                                                           in1=FKEEP[:, :], op0=ALU.is_gt, op1=ALU.add).then_inc(
                                fbit_done, 1)
                            dve.wait_ge(fbit_done, done + 6)
                            nc.vector.tensor_tensor(FROW[:, :], FROW[:, :], FKEEP[:, :], ALU.mult).then_inc(
                                fkeep_done, 1)
                    dve.wait_ge(flag_done, 1)
                if p == LAYER2:
                    def cut_e(i, s):
                        dve.wait_ge(ehi_ready, i + 1)
                        nc.vector.tensor_tensor(ELO[:, s, :, :], EW[:, s, :, :], EHI[:, s, :, :].bitcast(F32),
                                                ALU.subtract).then_inc(elo_ready, 1)

                    def add(i, t, k):
                        nc.vector.scalar_tensor_tensor(out=ACC[:, t, :], in0=pein[t % 4][:, k * F:(k + 1) * F],
                                                       scalar=column(NODE[:, t, :], 2 * i + k), in1=ACC[:, t, :],
                                                       op0=ALU.mult, op1=ALU.add).then_inc(ein_added, 1)

                    def group(i, s, more=True):
                        done = EIN_PRIME + i * 2 * T
                        for t in range(T):
                            if t == T // 3 and more:
                                cut_e(i + 1, 1 - s)
                            dve.wait_ge(ein_done, EIN_PRIME + i * T + t + 1)
                            dve.wait_ge(ein_added, done)
                            add(i, t, 0)
                            if t:
                                dve.wait_ge(ein_added, done + max(2 * t - 2, 1))
                                add(i, t - 1, 1)
                        dve.wait_ge(ein_added, done + 2 * T - 2)
                        add(i, T - 1, 1)
                    cut_e(0, 0)
                    for j in range(T):
                        dve.wait_ge(split_hi, T + j + 1)
                        nc.vector.tensor_tensor(lo_of(j), HN[:, j, :], hi_of(j).bitcast(F32), ALU.subtract).then_inc(
                            split_lo, 1)
                    dve.wait_ge(acc_zero, 1)
                    dve.wait_ge(dense_kept, 2 * T)
                    with dve.Fori(0, E_GROUPS // 2 - 1) as g:
                        group(2 * g, 0)
                        group(2 * g + 1, 1)
                    group(E_GROUPS - 2, 0)
                    group(E_GROUPS - 1, 1, more=False)
                early = p <= LAYER1
                if p in (LAYER1, LAYER2):
                    squared(p, first, 0)
                    squared(p, first, 1)
                    lo(p, first, 0)
                    for j in range(HB):
                        cut_h(p, j)
                    squared(p, first.next(), 0)
                    if early:
                        lo(p, first, 1)
                    node(p, first)
                    for j in range(HB, T):
                        cut_h(p, j)
                    weights_lo(p)

                def step(k):
                    old = beyond(k.t)
                    new = k.before(T - 1)
                    if old:
                        sums(p, k.prev())
                    if not early:
                        lo(p, k, 1)
                    if new:
                        squared(p, k.next(), 1)
                        positive(p, k.next(), 0)
                    if new and early:
                        lo(p, k.next(), 0)
                    if old:
                        scaled(p, k.prev())
                    if new:
                        if not early:
                            lo(p, k.next(), 0)
                        node(p, k.next())
                        positive(p, k.next(), 1)
                    if old:
                        turned(p, k.prev())
                    if k.before(T - 2):
                        squared(p, k.next().next(), 0)
                    if new and early:
                        lo(p, k.next(), 1)
                    if old:
                        dense(p, k.prev())
                tiles(dve, step)
                after = p + 1 if p + 1 in OVERLAP else None
                if after:
                    for j in range(HB):
                        cut_h(after, j)
                sums(p, LAST)
                if after:
                    lo(after, first, 0)
                scaled(p, LAST)
                turned(p, LAST)
                dense(p, LAST)
                if after:
                    for j in range(HB, T):
                        cut_h(after, j)
                    weights_lo(after)

        @block.tensor
        def _(pe):
            def cut_product(psum, lhs, rhs):
                for a in range(C):
                    for i, (l, r) in enumerate(((0, 0), (0, 1), (1, 0))):
                        mm = nc.tensor.matmul(psum, lhs(l, a), rhs(r, a), start=a == 0 and i == 0,
                                              stop=a == C - 1 and i == 2)
                return mm

            def part(p, k, q, low):
                n = 2 * T * p + 2 * k.t + q
                s = k.s
                end = q == 1

                def cut_is_there(j):
                    if p and isinstance(k.t, int) and k.t == 0:
                        pe.wait_ge(split_lo, cuts_before(p) + q * HB + j + 1)
                if not low:
                    pe.wait_ge(hi_ready, n + 1)
                    for j in range(HB):
                        lhs = HI[:, q, j * P:(j + 1) * P]
                        b = q * HB + j
                        cut_is_there(j)
                        begin = q == 0 and j == 0
                        if p == LAYER0:
                            nc.tensor.matmul(pacc[s][:, 0:F + 2], lhs, H[:, b, 0:F + 2], start=begin,
                                             stop=end and j == HB - 1)
                            mm = nc.tensor.matmul(pcross[s][:, 0:F], lhs, lo_of(b), start=begin,
                                                  stop=end and j == HB - 1)
                        else:
                            both = bass.AP(H, b * HC, [[T * HC, P], [F + ONE, 2], [1, F]])
                            mm = nc.tensor.matmul(pacc[s][:, :], lhs, both, start=begin, stop=end and j == HB - 1)
                    mm.then_inc(hi_used, 1)
                    if p == LAYER0:
                        pe.wait_ge(nz_ready, n + 1)
                        for j in range(HB):
                            mm = nc.tensor.matmul(pcnt[s][:, 0:2], NZ[:, q, j * P:(j + 1) * P], ONEB[:, :],
                                                  start=q == 0 and j == 0, stop=end and j == HB - 1)
                        mm.then_inc(nz_used, 1)
                else:
                    w = F + 2 if p == LAYER0 else F
                    pe.wait_ge(lo_ready, RAW_PRIME + n + 1)
                    for j in range(HB):
                        mm = nc.tensor.matmul(pacc[s][:, 0:w], LO[:, q, j * P:(j + 1) * P], H[:, q * HB + j, 0:w],
                                              start=False, stop=False, skip_group_check=True)
                    mm.then_inc(lo_used, 1)

            def turn(p, k):
                n = T * p + k.t
                if p == LAYER3C:
                    return
                pe.wait_ge(row_ready, n + 1)
                if beyond(n):
                    pe.wait_ge(htlo_ready, n)
                for a in range(C):
                    mm = nc.tensor.transpose(pt[:, a * P:(a + 1) * P], ROW[:, a * P:(a + 1) * P], IDN[:, :])
                mm.then_inc(rt_done, 1)

            cuts_of = {LAYER0: 3, LAYER1: 3, LAYER2: 4, LAYER3A: 5, LAYER3B: 6}
            w = (WHI, WLO)
            ht = (HTHI, HTLO)
            h2 = (H2HI, H2LO)

            def dense_a(p, k):
                n = T * p + k.t
                if p == LAYER3C:
                    return
                pe.wait_ge(htlo_ready, n + 1)
                pe.wait_ge(w_lo, cuts_of[p])
                if beyond(n):
                    pe.wait_ge(dense_kept, n)
                if p == LAYER0:
                    for b in range(C):
                        mm = cut_product(pd[:, b * P:(b + 1) * P], lambda l, a: w[l][:, a, b * P:(b + 1) * P],
                                         lambda r, a: ht[r][:, a * P:(a + 1) * P])
                    mm.then_inc(proj_done, 1)
                elif p == LAYER1:
                    cut_product(pd[:, 0:K], lambda l, a: ht[l][:, a * P:(a + 1) * P],
                                lambda r, a: (ENHI, ENLO)[r][:, a, :]).then_inc(dense_done, 1)
                else:
                    cut_product(pd[:, 0:F], lambda l, a: ht[l][:, a * P:(a + 1) * P],
                                lambda r, a: WONE_CUT[r][:, a, :]).then_inc(dense_done, 1)

            def dense_b(p, k):
                if p == LAYER0:
                    pe.wait_ge(h2lo_ready, k.t + 1)
                    cut_product(pd[:, F:2 * F], lambda l, a: h2[l][:, a * P:(a + 1) * P],
                                lambda r, a: w[r][:, a, F:2 * F]).then_inc(dense_done, 1)

            pe.wait_ge(w0_in, 48)
            for f in range(C):
                for a in range(C):
                    mm = nc.tensor.matmul(pd[:, f * F:(f + 1) * F], R[:, T - 4 + a, f * P:(f + 1) * P],
                                          R[:, T - 2 + a, :],
                                          start=a == 0, stop=a == C - 1)
            mm.then_inc(wc_done, 1)
            rows, hthi, htlo = [ROW, Y], [HTHI, H2HI], [HTLO, H2LO]

            def turn0(k):
                pe.wait_ge(row0_ready, k.t + 1)
                if beyond(k.t - 1):
                    pe.wait_ge(htlo0, k.t - 1)
                for a in range(C):
                    mm = nc.tensor.transpose(prow[k.s][:, a * P:(a + 1) * P], rows[k.s][:, a * P:(a + 1) * P],
                                             IDN[:, :])
                mm.then_inc(rt0_done, 1)

            def step0(k):
                if k.before(T - 1):
                    turn0(k.next())
                pe.wait_ge(htlo0, k.t + 1)
                if beyond(k.t - 1):
                    pe.wait_ge(h0_lo, k.t - 1)
                    pe.wait_ge(x0_added, k.t - 1)
                cut = (hthi[k.s], htlo[k.s])
                cut_product(pden[k.s][:, :], lambda l, a: cut[l][:, a * P:(a + 1) * P],
                            lambda r, a: w[r][:, a, :]).then_inc(dense0_done, 1)
            pe.wait_ge(ident_set, 4)
            turn0(Tile(0, 0))
            pe.wait_ge(w_lo, 1)
            tiles(pe, step0)
            pe.wait_ge(h0_lo, T)
            pe.wait_ge(x0_added, T)
            pe.wait_ge(ones_set, 2)
            pe.wait_ge(const_in, 48)

            for p in ALL:
                if p == LAYER1:
                    pe.wait_ge(flag_done, 1)
                    flag = pe.value_load(FLAG[0:1, 0:1], min_val=0, max_val=1)
                    with pe.If(flag):
                        with pe.Fori(0, T) as t:
                            pe.wait_ge(fkeep_done, t + 1)
                            for b in range(FBLOCKS):
                                if b >= 4:
                                    pe.wait_ge(fout_ready, FBLOCKS * t + b - 3)
                                for c in range(4 * b, min(4 * b + 4, T)):
                                    mm = nc.tensor.transpose(pturn[b % 4][:, (c % 4) * P:(c % 4 + 1) * P],
                                                             FROW[:, c * P:(c + 1) * P], IDN[:, :])
                                mm.then_inc(fturned, 1)
                    pe.wait_ge(flag_done, 1)
                if p == LAYER2:
                    pe.wait_ge(cnt_kept, T)

                    def group(i, s):
                        pe.wait_ge(elo_ready, i + 1)
                        for t in range(T):
                            last = t - 4 if t >= 4 else max(v for v in range(T) if v % 4 == t)
                            done = EIN_PRIME + (i - (t < 4)) * 2 * T
                            pe.wait_ge(split_lo, T + t + 1)
                            pe.wait_ge(ein_added, done + min(2 * last + 3, 2 * T))
                            left = (H[:, t, 0:F], lo_of(t))
                            cut_product(pein[t % 4][:, :], lambda l, a: left[l][:, a * P:(a + 1) * P],
                                        lambda r, a: (EHI, ELO)[r][:, s, a, :]).then_inc(ein_done, 1)
                    with pe.Fori(0, E_GROUPS // 2) as g:
                        group(2 * g, 0)
                        group(2 * g + 1, 1)

                def step(k):
                    n = T * p + k.t
                    if p == LAYER2:
                        pe.wait_ge(nst_ready, k.t + 1)
                        if beyond(k.t):
                            pe.wait_ge(ntt_ready, k.t)
                        nc.tensor.transpose(pnode[:, 0:P], NST[:, :], IDN[:, :]).then_inc(nt_done, 1)
                    if beyond(n - 1):
                        pe.wait_ge(sum_ready, n - 1)
                        if p == LAYER0:
                            pe.wait_ge(cnt_kept, k.t - 1)
                    part(p, k, 0, False)
                    part(p, k, 0, True)
                    if beyond(k.t - 1):
                        dense_b(p, k.prev().prev())
                    if p in OVERLAP and not beyond(k.t):
                        turn(p - 1, LAST)
                        dense_a(p - 1, LAST)
                    part(p, k, 1, False)
                    if beyond(k.t):
                        turn(p, k.prev())
                    if p == LAYER2:
                        pe.wait_ge(ntt_ready, k.t + 1)
                        nc.tensor.matmul(pacc[k.s][:, 0:F], NTT[:, :], NB[:, :], start=False, stop=False,
                                         skip_group_check=True)
                    part(p, k, 1, True)
                    if beyond(k.t):
                        dense_a(p, k.prev())
                tiles(pe, step)
                if p + 1 not in OVERLAP:
                    dense_b(p, LAST.prev())
                    turn(p, LAST)
                    dense_a(p, LAST)
                    dense_b(p, LAST)


def kernel(**inputs):
    import numpy as np
    import concourse.bacc as bacc
    from concourse.bass_utils import run_bass_kernel_spmd

    a = {k: np.asarray(v) for k, v in inputs.items()}
    x = np.zeros((NP, F), np.float32)
    x[:N] = a["x"]
    adj = np.zeros((NP, NP), np.float32)
    adj[:N, :N] = a["adj"]
    arrays = {
        "x": x.reshape(T, P, F).transpose(1, 0, 2).reshape(P, T * F),
        "adjn": adj.reshape(T, P, NP),
        "adjb": adj.reshape(T, P, T, P).transpose(0, 3, 2, 1).reshape(T, P, NP),
        "neigh_w": a["L0_gnn_neigh_W"],
        "lin_wt": a["L0_gnn_lin_W"].T,
        "w_proj": a["L1_gnn_W_proj"], "b_proj": a["L1_gnn_b_proj"].reshape(C, P).T,
        "w_gcn": a["L1_gnn_W_gcn"], "b_gcn": a["L1_gnn_b_gcn"],
        "e_w1": a["L2_gnn_W1"],
        "e_w2": a["L2_gnn_W2"].reshape(K // 2, 2, C, P, F).transpose(0, 3, 2, 1, 4).reshape(K // 2, P, C, 2 * F),
        "e_b": a["L2_gnn_b"],
        "w1": a["L3_gnn_W1"], "b1": a["L3_gnn_b1"], "w2": a["L3_gnn_W2"], "b2": a["L3_gnn_b2"],
        "w3": a["L3_gnn_W3"], "b3": a["L3_gnn_b3"],
        "g1": a["L3_gnn_g1"], "be1": a["L3_gnn_be1"], "g2": a["L3_gnn_g2"], "be2": a["L3_gnn_be2"],
        "g3": a["L3_gnn_g3"], "be3": a["L3_gnn_be3"],
    }
    nc = bacc.Bacc("TRN2", target_bir_lowering=False, num_devices=1)
    feed, args = {}, {}
    for name, array in arrays.items():
        array = np.ascontiguousarray(array)
        feed[f"in_{name}"] = array
        args[name] = nc.dram_tensor(f"in_{name}", array.shape, mybir.dt.from_np(array.dtype), kind="ExternalInput").ap()
    out = nc.dram_tensor("out", (T, P, F), F32, kind="ExternalOutput").ap()
    adjf = nc.dram_tensor("adj_top", (T, P, NP), F32, kind="Internal").ap()
    build(nc, out=out, adjf=adjf, **args)
    r = run_bass_kernel_spmd(nc, [feed], core_ids=[0])
    return r.results[0]["out"].reshape(NP, F)[:N]
```

```python
from contextlib import ExitStack

import concourse.bass as bass
from concourse import mybir

F32 = mybir.dt.float32
F32R = mybir.dt.float32r
BF16 = mybir.dt.bfloat16
I32 = mybir.dt.int32
ALU = mybir.AluOpType
ACT = mybir.ActivationFunctionType
AX = mybir.AxisListType

P = 128
N = 3327
T = (N + P - 1) // P
NP = T * P
F = 256
C = F // P
HB = T // 2
K = 32
TOP = 700
NBITS = 31
ONE = 4
HC = 2 * F + ONE
EPS = 1e-5
LAYER0, LAYER1, LAYER2, LAYER3A, LAYER3B, LAYER3C = range(6)
PRIME = 2
RAW_PRIME = 4
AHEAD = 6
TAIL = AHEAD + (T - 2 - AHEAD) % 4
EIN_PRIME = 2 * T


class Tile:

    def __init__(self, u, s):
        self.u, self.s = u, s
        self.t = 2 * u + s

    def next(self):
        return Tile(self.u, 1) if self.s == 0 else Tile(self.u + 1, 0)

    def prev(self):
        return Tile(self.u, 0) if self.s == 1 else Tile(self.u - 1, 1)

    def before(self, t):
        return not isinstance(self.t, int) or self.t < t


LAST = Tile(T // 2 - 1, 1)


def tiles(eng, step, tail=2, pairs=1, before_tail=None):
    step(Tile(0, 0))
    step(Tile(0, 1))
    with eng.Fori(0, (T - tail - 2) // (2 * pairs)) as v:
        for i in range(pairs):
            step(Tile(pairs * v + 1 + i, 0))
            step(Tile(pairs * v + 1 + i, 1))
    if before_tail:
        before_tail()
    for t in range(T - tail, T):
        step(Tile(t // 2, t % 2) if t < T - 1 else LAST)


def beyond(value):
    return not isinstance(value, int) or value > 0


def column(buf, t):
    return buf[:, t:t + 1] if isinstance(t, int) else buf[:, bass.ds(t, 1)]


def build(nc, x, adjn, adjb, adjf, neigh_w, lin_wt, w_proj, b_proj, w_gcn, b_gcn, e_w1, e_w2, e_b, w1, b1, w2, b2, w3, b3,
          g1, be1, g2, be2, g3, be3, out):
    with ExitStack() as ctx:
        def sb(name, shape, dt=F32):
            return ctx.enter_context(nc.sbuf_tensor(name, shape, dt))

        def sem(name):
            return ctx.enter_context(nc.semaphore(name))

        base = -(-nc.sbuf_base // 32) * 32
        X = sb("X", [P, T, F])
        H = sb("H", [P, T, HC], F32R)
        h_at = base + T * F * 4
        hn_at = h_at + T * HC * 4
        r_at = hn_at + T * F * 4
        HN = sb("HN", [P, T, F])
        R = sb("R", [P, T, F])
        ring_at = r_at + T * F * 4
        half = HB * P
        RAW = sb("RAW", [P, 2, half])
        HI = sb("HI", [P, 2, half], F32R)
        LO = sb("LO", [P, 2, half], F32R)
        def at(name, shape, dt, offset):
            return nc.alloc_sbuf_tensor_at(name, shape, dt, offset=offset)

        NZ = at("NZ", [P, 2, half], BF16, r_at)
        RAWX = at("RAWX", [P, 2, half], F32, r_at + 4 * half)
        ACC = at("ACC", [P, T, F], F32, r_at)
        hi_at = ring_at + 8 * half
        EW = at("EW", [P, 2, C, 2 * F], F32, hi_at)
        EHI, ELO = ([at(f"E{part}{s}", [P, C, 2 * F], F32R, hi_at + 8 * F * C * (2 + 2 * s + i)) for s in range(2)]
                    for i, part in enumerate(("HI", "LO")))
        FROW = at("FROW", [P, NP], F32, h_at)
        FVAL = at("FVAL", [P, NP], F32, h_at + 4 * NP)
        FTMP = at("FTMP", [P, NP], F32, h_at + 8 * NP)
        FKEEP = at("FKEEP", [P, NP], F32, h_at + 12 * NP)
        early_at = -(-nc.sbuf_base // 32) * 32
        W = sb("W", [P, C, 2 * F])
        H2 = sb("H2", [P, F])
        H2HI = sb("H2HI", [P, F], F32R)
        H2LO = sb("H2LO", [P, F], F32R)
        WLO = sb("WLO", [P, C, 2 * F], F32R)
        EN = sb("EN", [P, C, K])
        ENHI = sb("ENHI", [P, C, K], F32R)
        ENLO = sb("ENLO", [P, C, K], F32R)
        SPARE = sb("SPARE", [P, half - (C * 2 * F + 3 * C * K)])
        RAWY = at("RAWY", [P, half], F32, early_at)
        RAWZ = at("RAWZ", [P, half], F32, early_at + 4 * (C * 2 * F + 3 * F))
        WHI = sb("WHI", [P, C, 2 * F], F32R)
        WONE = sb("WONE", [P, C, F])
        WONE_CUT = (WHI[:, 0, :].rearrange("p (a f) -> p a f", a=C), WHI[:, 1, :].rearrange("p (a f) -> p a f", a=C))
        BIAS = sb("BIAS", [P, F])
        GAIN = sb("GAIN", [P, F])
        SHIFT = sb("SHIFT", [P, F])
        BPC = sb("BPC", [P, C])
        NB = sb("NB", [P, F])
        CROSS = sb("CROSS", [P, F])
        SUM = sb("SUM", [P, F])
        SUM2 = sb("SUM2", [P, F])
        CMAX = sb("CMAX", [P, 1])
        CALL = sb("CALL", [P, 1])
        FLAG = sb("FLAG", [P, 1], I32)
        BITS = sb("BITS", [P, NBITS], I32)
        VBITS = sb("VBITS", [P, 1], I32)
        CAND = sb("CAND", [P, 1], I32)
        TAKE = sb("TAKE", [P, 1], I32)
        FCNT = sb("FCNT", [P, 1])
        ROOM = sb("ROOM", [P, 1])
        Y = sb("Y", [P, F])
        ROW = sb("ROW", [P, F])
        HTHI = sb("HTHI", [P, F], F32R)
        HTLO = sb("HTLO", [P, F], F32R)
        NODE = sb("NODE", [P, T, K])
        NST = sb("NST", [P, P])
        NTT = sb("NTT", [P, P])
        IDN = sb("IDN", [P, P])
        ONEB = sb("ONEB", [P, 2], BF16)
        DEG = sb("DEG", [P, T])
        CNT = sb("CNT", [P, T])
        PAD = sb("PAD", [P, T])
        DINV = sb("DINV", [P, T])
        RDEG = sb("RDEG", [P, 1])
        HALF = sb("HALF", [P, T])
        MINUS = sb("MINUS", [P, 1])
        EPSC = sb("EPSC", [P, 1])
        IDLE = sb("IDLE", [P, 2])
        ST = sb("ST", [P, 6])
        ST0 = sb("ST0", [P, 2, 6])
        MV = sb("MV", [P, 2])
        MV0 = sb("MV0", [P, 2, 2])
        NM0 = sb("NM0", [P, T])
        VE = sb("VE", [P, T])
        RSTD = sb("RSTD", [P, T])
        NMR = sb("NMR", [P, T])
        NM = sb("NM", [P, 1])

        bank = [ctx.enter_context(nc.psum_tensor(f"bank{i}", [P, 512], F32)) for i in range(8)]
        pacc = bank[0:2]
        pt = bank[2]
        pd = bank[3]
        pcnt = bank[4:6]
        pcross = bank[6:8]
        pnode = bank[6]
        pturn = bank[4:6]
        pein = bank[4:8]
        prow = [bank[2], bank[4]]
        pden = [bank[3], bank[5]]

        x_in = [sem("x_in0"), sem("x_in1")]
        const_in, w0_in, par_in = sem("const_in"), sem("w0_in"), sem("par_in")
        nb_set, pool_set, ones_set, ident_set = sem("nb_set"), sem("pool_set"), sem("ones_set"), sem("ident_set")
        wc_done, wc_kept, w_hi, w_lo = sem("wc_done"), sem("wc_kept"), sem("w_hi"), sem("w_lo")
        st0_done, mv0_done, ve0_done, nm0_done, rstd0_done, nmr0_done = (
            sem("st0_done"), sem("mv0_done"), sem("ve0_done"), sem("nm0_done"), sem("rstd0_done"), sem("nmr0_done"))
        row0_ready, rt0_done, hthi0, htlo0, dense0_done, h0_hi, h0_lo, x0_added = (
            sem("row0_ready"), sem("rt0_done"), sem("hthi0"), sem("htlo0"), sem("dense0_done"), sem("h0_hi"),
            sem("h0_lo"), sem("x0_added"))
        raw_in = [sem(f"raw_in{i}") for i in range(4)]
        hi_ready, lo_ready, hi_used, lo_used = sem("hi_ready"), sem("lo_ready"), sem("hi_used"), sem("lo_used")
        nz_ready, nz_used = sem("nz_ready"), sem("nz_used")
        sq_ready, th_ready = sem("sq_ready"), sem("th_ready")
        cross_ready, sum_ready, sum2_ready, y_ready = (
            sem("cross_ready"), sem("sum_ready"), sem("sum2_ready"), sem("y_ready"))
        deg_kept, deg1_kept, rdeg_kept, cnt_kept = sem("deg_kept"), sem("deg1_kept"), sem("rdeg_kept"), sem("cnt_kept")
        st_done, mv_done, ve_done, rstd_done, nm_done, nmr_done = (
            sem("st_done"), sem("mv_done"), sem("ve_done"), sem("rstd_done"), sem("nm_done"), sem("nmr_done"))
        z_ready, zg_ready = sem("z_ready"), sem("zg_ready")
        row_ready, row_kept = sem("row_ready"), sem("row_kept")
        rt_done, hthi_ready, htlo_ready = sem("rt_done"), sem("hthi_ready"), sem("htlo_ready")
        ht_kept, crossb_ready = sem("ht_kept"), sem("crossb_ready")
        cmax_done, call_done, flag_done, bits_set = sem("cmax_done"), sem("call_done"), sem("flag_done"), sem("bits_set")
        frow_in, fsq_done, fval_done, fbit_done, fkeep_done, fturned, fout_ready, fout_done, frow_again = (
            sem("frow_in"), sem("fsq_done"), sem("fval_done"), sem("fbit_done"), sem("fkeep_done"), sem("fturned"),
            sem("fout_ready"), sem("fout_done"), sem("frow_again"))
        proj_done, tanh_done, h2hi_ready, h2lo_ready = (
            sem("proj_done"), sem("tanh_done"), sem("h2hi_ready"), sem("h2lo_ready"))
        dense_done, dense_kept = sem("dense_done"), sem("dense_kept")
        nst_ready, nt_done, ntt_ready = sem("nst_ready"), sem("nt_done"), sem("ntt_ready")
        dinv_pad, dinv_done = sem("dinv_pad"), sem("dinv_done")
        split_hi, split_lo, split_lo_pool = sem("split_hi"), sem("split_lo"), sem("split_lo_pool")
        ew_in = [sem("ew_in0"), sem("ew_in1")]
        ehi_ready, elo_ready = sem("ehi_ready"), sem("elo_ready")
        ein_done, ein_added = sem("ein_done"), sem("ein_added")
        out_ready, out_done = sem("out_ready"), sem("out_done")

        block = ctx.enter_context(nc.Block())

        def past(p, phases):
            return T * len([q for q in phases if q < p])

        ALL = range(6)
        DENSE = (LAYER0, LAYER1, LAYER2, LAYER3A, LAYER3B)
        L3 = (LAYER3A, LAYER3B, LAYER3C)
        E_GROUPS = K // 2
        FBLOCKS = -(-T // 4)

        def raw_of(p, k, q):
            if k.s == 0:
                return RAW[:, q, :]
            return RAWX[:, q, :] if p <= LAYER1 else (RAWY, RAWZ)[q][:, :]

        def raw_landed(p, k):
            return 16 * (T // 2 * p + k.u + 1)

        def main_of(p, s):
            return pacc[s][:, 0:F]

        def cross_of(p, s):
            return pcross[s][:, 0:F] if p == LAYER0 else pacc[s][:, F:2 * F]

        def hi_of(j):
            return H[:, j, 0:F]

        def lo_of(j):
            return H[:, j, F + ONE:HC]

        def cuts_before(p):
            return 0 if p == LAYER1 else T * p

        FIRST_CUTS = 5

        def by_pool(p):
            return list(range(7)) if p == LAYER1 else []

        def low_parts(p, j):
            pool = j in by_pool(p)
            before = sum(len(by_pool(q)) for q in range(p))
            same = len([i for i in range(j + 1) if (i in by_pool(p)) == pool])
            return (split_lo_pool, before + same) if pool else (split_lo, cuts_before(p) - before + same)

        def cut_source(p):
            return {LAYER1: HN, LAYER2: ACC, LAYER3A: R, LAYER3B: HN, LAYER3C: HN}[p]

        OVERLAP = (LAYER1, LAYER3A, LAYER3B, LAYER3C)

        def weight(w, k=None):
            return WONE[:, :, :] if k is None else W[:, :, k * F:(k + 1) * F], w.rearrange("(a p) f -> p a f", p=P)

        def spread(buf, v):
            return buf[:, :], v.rearrange("(a f) -> a f", a=1).to_broadcast([P, F])

        loads_of = {
            LAYER0: [weight(w_proj, 0), weight(w_gcn, 1)],
            LAYER1: [spread(BIAS, b_gcn)],
            LAYER2: [weight(w1), spread(BIAS, b1)],
            LAYER3A: [weight(w2), spread(BIAS, b2), spread(GAIN, g1), spread(SHIFT, be1)],
            LAYER3B: [weight(w3), spread(BIAS, b3), spread(GAIN, g2), spread(SHIFT, be2)],
            LAYER3C: [spread(GAIN, g3), spread(SHIFT, be3)],
        }

        def par_count(p):
            return 16 * sum(len(loads_of[q]) for q in range(p + 1))

        @block.sync
        def _(sp):
            def load(p, k, source):
                for q in range(2):
                    n = 2 * T * p + 2 * k.t + q
                    sp.wait_ge(lo_ready, n + 1)
                    sp.dma_start(raw_of(p, k, q), source[k.t, :, q * half:(q + 1) * half]).then_inc(
                        raw_in[2 * k.s + q], 16)

            def load_all(p, source, first=0):
                with sp.Fori(first, T // 2) as u:
                    load(p, Tile(u, 0), source)
                    load(p, Tile(u, 1), source)

            sp.dma_start(R[:, T - 4:T - 2, :], neigh_w.rearrange("(a p) f -> p a f", p=P)).then_inc(w0_in, 16)
            sp.dma_start(R[:, T - 2:T, :], lin_wt[F:2 * F, :].rearrange("(a p) f -> p a f", p=P)).then_inc(w0_in, 16)
            sp.dma_start(W[:, :, F:2 * F], lin_wt[0:F, :].rearrange("(a p) f -> p a f", p=P)).then_inc(w0_in, 16)
            xs = x.rearrange("p (t f) -> p t f", t=T)
            sp.dma_start(X[:, 0:AHEAD, :], xs[:, 0:AHEAD, :]).then_inc(x_in[0], 16)
            sp.dma_start(X[:, AHEAD:T, :], xs[:, AHEAD:T, :]).then_inc(x_in[1], 16)
            load(LAYER0, Tile(0, 0), adjb)
            sp.dma_start(EN[:, :, :], e_w1.rearrange("(a p) k -> p a k", p=P)).then_inc(const_in, 16)
            sp.dma_start(BPC[:, :], b_proj).then_inc(const_in, 16)
            sp.wait_ge(nb_set, 1)
            sp.dma_start(NB[0:K, :], e_b).then_inc(const_in, 16)
            load(LAYER0, Tile(0, 1), adjb)
            load_all(LAYER0, adjb, 1)

            load(LAYER1, Tile(0, 0), adjb)
            load(LAYER1, Tile(0, 1), adjb)
            sp.wait_ge(flag_done, 1)
            flag = sp.value_load(FLAG[0:1, 0:1], min_val=0, max_val=1)
            with sp.If(flag):
                sp.wait_ge(lo_used, PRIME + 2 * T)
                with sp.Fori(0, T) as t:
                    sp.wait_ge(fout_done, 16 * (t + 1))
                    sp.dma_start(FROW[:, :], adjn[t]).then_inc(frow_in, 16)
                    sp.wait_ge(fout_ready, FBLOCKS * (t + 1))
                    sp.dma_start(adjf[t], FTMP[:, :]).then_inc(fout_done, 16)
                sp.wait_ge(fout_done, 16 * (T + 1))
                for s in range(2):
                    for q in range(2):
                        sp.wait_ge(raw_in[2 * s + q], raw_landed(LAYER1, Tile(0, s)))
                        sp.dma_start(raw_of(LAYER1, Tile(0, s), q), adjf[s, :, q * half:(q + 1) * half]).then_inc(
                            frow_again, 16)
                load_all(LAYER1, adjf, 1)
            with sp.Else():
                load_all(LAYER1, adjb, 1)

            sp.wait_ge(lo_ready, RAW_PRIME + 2 * T * LAYER2 - 1)
            sp.wait_ge(hi_used, PRIME + 2 * T * LAYER2 - 1)
            sp.dma_start(EW[:, 0, :, :], e_w2[0]).then_inc(ew_in[0], 16)
            sp.wait_ge(lo_ready, RAW_PRIME + 2 * T * LAYER2)
            sp.wait_ge(hi_used, PRIME + 2 * T * LAYER2)
            sp.dma_start(EW[:, 1, :, :], e_w2[1]).then_inc(ew_in[1], 16)
            with sp.Fori(1, E_GROUPS // 2) as g:
                for s in range(2):
                    sp.wait_ge(elo_ready, 2 * g + s - 1)
                    sp.dma_start(EW[:, s, :, :], e_w2[2 * g + s]).then_inc(ew_in[s], 16)
            sp.wait_ge(dense_done, T * LAYER2)
            for p in (LAYER2, LAYER3A, LAYER3B, LAYER3C):
                load_all(p, adjb)

        @block.gpsimd
        def _(pool):
            nc.gpsimd.memset(NB[:, :], 0.0).then_inc(nb_set, 1)
            nc.gpsimd.memset(IDN[:, :], 0.0).then_inc(ident_set, 1)
            nc.gpsimd.memset(PAD[:, :], 0.0).then_inc(ident_set, 1)
            nc.gpsimd.memset(HALF[:, :], -0.5).then_inc(pool_set, 1)
            nc.gpsimd.memset(NST[:, :], 0.0).then_inc(pool_set, 1)
            nc.gpsimd.memset(MINUS[:, :], -1.0).then_inc(pool_set, 1)
            nc.gpsimd.memset(EPSC[:, :], EPS).then_inc(pool_set, 1)
            pool.wait_ge(ident_set, 2)
            nc.gpsimd.affine_select(out=IDN[:, :], in_=IDN[:, :], compare_op=ALU.not_equal, fill=1.0, base=0,
                                    pattern=[[-1, P]], channel_multiplier=1).then_inc(ident_set, 1)
            nc.gpsimd.affine_select(out=PAD[:, :], in_=PAD[:, :], compare_op=ALU.is_gt, fill=1.0, base=N,
                                    pattern=[[-P, T]], channel_multiplier=-1).then_inc(ident_set, 1)
            for b in range(NBITS):
                nc.gpsimd.memset(BITS[:, b:b + 1], 1 << (NBITS - 1 - b)).then_inc(bits_set, 1)
            pool.wait_ge(pool_set, 4)

            def norm0(k):
                pool.wait_ge(mv0_done, k.t + 1)
                nc.gpsimd.tensor_tensor(column(VE, k.t), MV0[:, k.s, 1:2], EPSC[:, :], ALU.add).then_inc(ve0_done, 1)
                nc.gpsimd.tensor_tensor(column(NM0, k.t), MV0[:, k.s, 0:1], MINUS[:, :], ALU.mult).then_inc(nm0_done, 1)
                pool.wait_ge(ve0_done, k.t + 1)
                nc.gpsimd.tensor_tensor(column(RSTD, k.t), column(VE, k.t), HALF[:, 0:1], ALU.pow).then_inc(rstd0_done, 1)
                pool.wait_ge(rstd0_done, k.t + 1)
                pool.wait_ge(nm0_done, k.t + 1)
                nc.gpsimd.tensor_tensor(column(NMR, k.t), column(NM0, k.t), column(RSTD, k.t), ALU.mult).then_inc(
                    nmr0_done, 1)
            tiles(pool, norm0, TAIL, 2)

            for p in ALL:
                def norm(k):
                    n = T * p + k.t
                    if p == LAYER0 and k is LAST:
                        pool.wait_ge(cmax_done, 1)
                        nc.gpsimd.partition_all_reduce(CALL[:, :], CMAX[:, :], P, bass.bass_isa.ReduceOp.max).then_inc(
                            call_done, 1)
                        for j in by_pool(LAYER1):
                            pool.wait_ge(split_hi, j + 1)
                            nc.gpsimd.tensor_tensor(lo_of(j), HN[:, j, :], hi_of(j).bitcast(F32), ALU.subtract).then_inc(
                                split_lo_pool, 1)
                    if p == LAYER1 and isinstance(k.t, int) and k.t == 1:
                        pool.wait_ge(deg_kept, T)
                        pool.wait_ge(ident_set, 4)
                        nc.gpsimd.tensor_tensor(DEG[:, :], DEG[:, :], PAD[:, :], ALU.add).then_inc(dinv_pad, 1)
                        pool.wait_ge(dinv_pad, 1)
                        nc.gpsimd.tensor_tensor(DINV[:, :], DEG[:, :], HALF[:, :], ALU.pow).then_inc(dinv_done, 1)
                    if p == LAYER1:
                        pool.wait_ge(par_in, par_count(p))
                        pool.wait_ge(cross_ready, n + 1)
                        nc.gpsimd.tensor_tensor(CROSS[:, :], CROSS[:, :], BIAS[:, :], ALU.add).then_inc(crossb_ready, 1)
                    pool.wait_ge(mv_done, n + 1)
                    nc.gpsimd.tensor_tensor(VE[:, 0:1], MV[:, 1:2], EPSC[:, :], ALU.add).then_inc(ve_done, 1)
                    pool.wait_ge(ve_done, n + 1)
                    if beyond(n):
                        pool.wait_ge(row_ready, n)
                    nc.gpsimd.tensor_tensor(RSTD[:, 0:1], VE[:, 0:1], HALF[:, 0:1], ALU.pow).then_inc(rstd_done, 1)
                    pool.wait_ge(rstd_done, n + 1)
                    nc.gpsimd.tensor_tensor(NM[:, :], MV[:, 0:1], MINUS[:, :], ALU.mult).then_inc(nm_done, 1)
                    pool.wait_ge(nm_done, n + 1)
                    nc.gpsimd.tensor_tensor(NMR[:, 0:1], NM[:, :], RSTD[:, 0:1], ALU.mult).then_inc(nmr_done, 1)
                    if p == LAYER1:
                        pool.wait_ge(htlo_ready, n + 1)
                        nc.gpsimd.tensor_tensor(HN[:, k.t, :], HTHI[:, :].bitcast(F32), HTLO[:, :].bitcast(F32),
                                                ALU.add).then_inc(ht_kept, 1)
                tiles(pool, norm)

        @block.scalar
        def _(act):
            act.sem_inc(lo_ready, RAW_PRIME)
            act.sem_inc(hi_used, PRIME)
            act.sem_inc(lo_used, PRIME)
            act.sem_inc(nz_used, PRIME)
            act.sem_inc(fout_done, 16)
            act.sem_inc(ein_done, EIN_PRIME)
            act.sem_inc(ein_added, EIN_PRIME)

            def squashed(p, k, q):
                if p == LAYER1:
                    raw = raw_of(p, k, q)
                    act.wait_ge(sq_ready, 2 * k.t + q + 1)
                    nc.scalar.activation(raw, raw, ACT.Tanh).then_inc(th_ready, 1)

            def hi(p, k, q):
                n = 2 * T * p + 2 * k.t + q
                if p == LAYER1:
                    act.wait_ge(th_ready, 2 * k.t + q + 1)
                else:
                    act.wait_ge(raw_in[2 * k.s + q], raw_landed(p, k))
                act.wait_ge(hi_used, n + 1)
                act.wait_ge(lo_ready, n + 3)
                nc.scalar.activation(HI[:, q, :], raw_of(p, k, q), ACT.Copy).then_inc(hi_ready, 1)

            def cross(p, k):
                n = T * p + k.t
                act.wait_ge(lo_used, PRIME + 2 * (n + 1))
                if beyond(n):
                    act.wait_ge(sum_ready, n)
                nc.scalar.activation(CROSS[:, :], cross_of(p, k.s), ACT.Copy).then_inc(cross_ready, 1)

            def row(p, k):
                n = T * p + k.t
                if p < LAYER3A:
                    act.wait_ge(nmr_done, n + 1)
                    if beyond(n):
                        act.wait_ge(rt_done, n)
                    nc.scalar.activation(ROW[:, :], X[:, k.t, :], ACT.Relu, bias=NMR[:, 0:1],
                                         scale=RSTD[:, 0:1]).then_inc(row_ready, 1)
                elif p < LAYER3C:
                    act.wait_ge(row_ready, n + 1)
                    nc.scalar.activation(R[:, k.t, :], ROW[:, :], ACT.Copy).then_inc(row_kept, 1)

            def turned(p, k):
                n = T * p + k.t
                if p == LAYER3C:
                    return
                act.wait_ge(rt_done, n + 1)
                if beyond(n):
                    act.wait_ge(dense_done, n)
                if p == LAYER1 and beyond(k.t):
                    act.wait_ge(ht_kept, k.t)
                nc.scalar.activation(HTHI[:, :], pt[:, 0:F], ACT.Copy).then_inc(hthi_ready, 1)

            def dense_1(p, k):
                n = T * p + k.t
                if p == LAYER0:
                    act.wait_ge(proj_done, k.t + 1)
                    for a in range(C):
                        nc.scalar.activation(H2[:, a * P:(a + 1) * P], pd[:, a * P:(a + 1) * P], ACT.Tanh,
                                             bias=BPC[:, a:a + 1]).then_inc(tanh_done, 1)
                    act.wait_ge(tanh_done, 2 * k.t + 2)
                    if beyond(k.t):
                        act.wait_ge(dense_done, k.t)
                    nc.scalar.activation(H2HI[:, :], H2[:, :], ACT.Copy).then_inc(h2hi_ready, 1)
                if p == LAYER1:
                    act.wait_ge(dense_done, n + 1)
                    nc.scalar.activation(NODE[:, k.t, :], pd[:, 0:K], ACT.Copy).then_inc(dense_kept, 1)
                if p == LAYER3C:
                    act.wait_ge(out_ready, k.t + 1)
                    act.dma_start(out[k.t], X[:, k.t, :]).then_inc(out_done, 16)

            def dense_2(p, k):
                if p == LAYER0:
                    act.wait_ge(dense_done, k.t + 1)
                    nc.scalar.activation(HN[:, k.t, :], pd[:, F:2 * F], ACT.Copy).then_inc(dense_kept, 1)

            def cut_h(p, j):
                act.wait_ge(lo_used, PRIME + 2 * T * p - (j < HB))
                src = cut_source(p)
                if p == LAYER2:
                    act.wait_ge(ein_added, EIN_PRIME + 2 * T * (E_GROUPS - 1) + min(2 * j + 3, 2 * T))
                    act.wait_ge(ein_done, EIN_PRIME + T * (E_GROUPS - 1) + j + 1)
                else:
                    act.wait_ge(dense_kept, T * (p - 1) + j + 1)
                if p in L3:
                    nc.scalar.activation(hi_of(j), src[:, j, :], ACT.Copy, scale=DINV[:, j:j + 1]).then_inc(split_hi, 1)
                else:
                    nc.scalar.activation(hi_of(j), src[:, j, :], ACT.Copy).then_inc(split_hi, 1)

            def cut_some(p, j0, j1):
                for j in range(j0, j1):
                    cut_h(p, j)

            def params(p):
                if p == LAYER0:
                    act.wait_ge(dense0_done, T)
                    act.wait_ge(w_lo, 1)
                else:
                    act.wait_ge(row_ready, T * p)
                    act.wait_ge(dense_done, past(p, DENSE))
                    act.wait_ge(dense_kept, past(p, DENSE))
                for dst, src in loads_of[p]:
                    act.dma_start(dst, src).then_inc(par_in, 16)

            def weights_hi(p):
                if p not in (LAYER1, LAYER3C):
                    act.wait_ge(par_in, par_count(p))
                    whole, high = (W, WHI) if p == LAYER0 else (WONE, WONE_CUT[0])
                    nc.scalar.activation(high[:, :, :], whole[:, :, :], ACT.Copy).then_inc(w_hi, 1)

            act.wait_ge(wc_done, 1)
            act.wait_ge(w0_in, 48)
            nc.scalar.activation(W[:, :, 0:F], pd[:, :].rearrange("p (a f) -> p a f", a=C), ACT.Copy).then_inc(wc_kept, 1)
            act.wait_ge(wc_kept, 1)
            nc.scalar.activation(WHI[:, :, :], W[:, :, :], ACT.Copy).then_inc(w_hi, 1)

            rows, hthi = [ROW, Y], [HTHI, H2HI]

            def row0(k):
                act.wait_ge(nmr0_done, k.t + 1)
                if beyond(k.t - 1):
                    act.wait_ge(rt0_done, k.t - 1)
                nc.scalar.activation(rows[k.s][:, :], X[:, k.t, :], ACT.Relu, bias=column(NMR, k.t),
                                     scale=column(RSTD, k.t)).then_inc(row0_ready, 1)

            def turned0(k):
                act.wait_ge(rt0_done, k.t + 1)
                if beyond(k.t - 1):
                    act.wait_ge(dense0_done, k.t - 1)
                nc.scalar.activation(hthi[k.s][:, :], prow[k.s][:, 0:F], ACT.Copy).then_inc(hthi0, 1)

            def keep0(k):
                act.wait_ge(dense0_done, k.t + 1)
                nc.scalar.activation(hi_of(k.t), pden[k.s][:, 0:F], ACT.Copy).then_inc(h0_hi, 1)

            def step0(k):
                if k.before(T - 1):
                    turned0(k.next())
                if beyond(k.t):
                    keep0(k.prev())
                if k.before(T - 3):
                    row0(k.next().next().next())
            first = Tile(0, 0)
            row0(first)
            row0(first.next())
            turned0(first)
            row0(first.next().next())
            tiles(act, step0, TAIL, 2, lambda: hi(LAYER0, first, 0))
            keep0(LAST)
            hi(LAYER0, first, 1)
            act.wait_ge(const_in, 48)
            nc.scalar.activation(ENHI[:, :, :], EN[:, :, :], ACT.Copy).then_inc(w_hi, 1)
            params(LAYER0)
            weights_hi(LAYER0)

            def general():
                act.wait_ge(flag_done, 1)
                flag = act.value_load(FLAG[0:1, 0:1], min_val=0, max_val=1)
                with act.If(flag):
                    with act.Fori(0, T) as t:
                        act.wait_ge(fsq_done, t + 1)
                        nc.scalar.activation(FVAL[:, :], FTMP[:, :], ACT.Tanh).then_inc(fval_done, 1)
                        for b in range(FBLOCKS):
                            w = min(4 * P, NP - 4 * P * b)
                            act.wait_ge(fturned, FBLOCKS * t + b + 1)
                            nc.scalar.activation(FTMP[:, 4 * P * b:4 * P * b + w], pturn[b % 2][:, 0:w],
                                                 ACT.Copy).then_inc(fout_ready, 1)
                act.wait_ge(flag_done, 1)

            for p in ALL:
                def into_layer2():
                    def cut_turned(j0, j1):
                        for j in range(j0, j1):
                            act.wait_ge(ht_kept, j + 1)
                            act.wait_ge(lo_used, PRIME + 2 * T * LAYER2 - (j < HB))
                            nc.scalar.activation(hi_of(j), HN[:, j, :], ACT.Copy).then_inc(split_hi, 1)

                    def cut_e(g, s):
                        act.wait_ge(ew_in[s], 16 * (g + 1))
                        act.wait_ge(ein_done, T * (2 * g + s + 1))
                        nc.scalar.activation(EHI[s][:, :, :], EW[:, s, :, :], ACT.Copy).then_inc(ehi_ready, 1)
                    prev = LAST.prev()
                    cross(LAYER1, prev)
                    row(LAYER1, prev)
                    cut_turned(0, FIRST_CUTS)
                    turned(LAYER1, prev)
                    act.wait_ge(hi_used, PRIME + 2 * T * LAYER2)
                    act.wait_ge(lo_ready, RAW_PRIME + 2 * T * LAYER2)
                    cut_e(0, 0)
                    cross(LAYER1, LAST)
                    dense_1(LAYER1, prev)
                    cut_turned(FIRST_CUTS, HB)
                    row(LAYER1, LAST)
                    cut_turned(HB, HB + 4)
                    turned(LAYER1, LAST)
                    cut_turned(HB + 4, T - 1)
                    dense_1(LAYER1, LAST)
                    cut_turned(T - 1, T)
                    params(LAYER2)
                    weights_hi(LAYER2)
                    act.wait_ge(lo_used, PRIME + 2 * T * LAYER2)
                    cut_e(0, 1)
                    with act.Fori(1, E_GROUPS // 2) as g:
                        cut_e(g, 0)
                        cut_e(g, 1)
                    act.wait_ge(elo_ready, E_GROUPS)
                    act.wait_ge(ein_done, EIN_PRIME + T * (E_GROUPS - 1))
                    hi(LAYER2, first, 0)
                    hi(LAYER2, first, 1)
                    cut_some(LAYER2, 0, T)

                def into_layer1():
                    prev = LAST.prev()
                    cross(LAYER0, prev)
                    dense_2(LAYER0, prev.prev())
                    row(LAYER0, prev)
                    general()
                    cut_some(LAYER1, 0, len(by_pool(LAYER1)))
                    squashed(LAYER1, first, 0)
                    turned(LAYER0, prev)
                    hi(LAYER1, first, 0)
                    cross(LAYER0, LAST)
                    cut_some(LAYER1, len(by_pool(LAYER1)), HB)
                    dense_1(LAYER0, prev)
                    squashed(LAYER1, first, 1)
                    hi(LAYER1, first, 1)
                    cut_some(LAYER1, HB, HB + 6)
                    row(LAYER0, LAST)
                    dense_2(LAYER0, prev)
                    cut_some(LAYER1, HB + 6, HB + 8)
                    turned(LAYER0, LAST)
                    cut_some(LAYER1, HB + 8, T - 1)
                    dense_1(LAYER0, LAST)
                    dense_2(LAYER0, LAST)
                    cut_some(LAYER1, T - 1, T)
                    params(LAYER1)

                def step(k):
                    if p == LAYER0 and k is LAST:
                        into_layer1()
                        return
                    if p == LAYER1 and k is LAST:
                        into_layer2()
                        return
                    if p == LAYER2:
                        act.wait_ge(nt_done, k.t + 1)
                        nc.scalar.activation(NTT[:, :], pnode[:, 0:P], ACT.Copy).then_inc(ntt_ready, 1)
                    old = beyond(k.t)
                    new = k.before(T - 1)
                    if old:
                        cross(p, k.prev())
                    if new:
                        squashed(p, k.next(), 0)
                        hi(p, k.next(), 0)
                    if beyond(k.t - 1):
                        dense_2(p, k.prev().prev())
                    if old:
                        row(p, k.prev())
                    if new:
                        squashed(p, k.next(), 1)
                    if old:
                        turned(p, k.prev())
                    if new:
                        hi(p, k.next(), 1)
                    if old:
                        dense_1(p, k.prev())
                    elif p in L3:
                        weights_hi(p)
                tiles(act, step)
                if p <= LAYER1:
                    continue
                after = p + 1 if p + 1 in OVERLAP else None
                if after:
                    hi(after, first, 0)
                    cut_some(after, 0, HB - 3)
                cross(p, LAST)
                if after:
                    cut_some(after, HB - 3, HB)
                    hi(after, first, 1)
                    cut_some(after, HB, HB + 6)
                row(p, LAST)
                if after:
                    cut_some(after, HB + 6, T - 4)
                turned(p, LAST)
                dense_1(p, LAST)
                if after:
                    cut_some(after, T - 4, T)
                    params(after)
            act.wait_ge(out_done, 16 * T)

        @block.vector
        def _(dve):
            nc.vector.memset(H[:, :, F:F + ONE].bitcast(F32), 1.0).then_inc(ones_set, 1)
            nc.vector.memset(ONEB[:, :], 1.0).then_inc(ones_set, 1)

            def positive(p, k, q):
                if p == LAYER0:
                    n = 2 * k.t + q
                    dve.wait_ge(raw_in[2 * k.s + q], raw_landed(p, k))
                    dve.wait_ge(nz_used, n + 1)
                    nc.vector.tensor_scalar(NZ[:, q, :], raw_of(p, k, q), 0.0, None, ALU.is_gt).then_inc(nz_ready, 1)

            def squared(p, k, q):
                if p == LAYER1:
                    raw = raw_of(p, k, q)
                    dve.wait_ge(raw_in[2 * k.s + q], raw_landed(p, k))
                    nc.vector.scalar_tensor_tensor(out=raw, in0=raw, scalar=0.0, in1=raw, op0=ALU.max,
                                                   op1=ALU.mult).then_inc(sq_ready, 1)

            def lo(p, k, q):
                n = 2 * T * p + 2 * k.t + q
                dve.wait_ge(hi_ready, n + 1)
                dve.wait_ge(lo_used, n + 1)
                nc.vector.tensor_tensor(LO[:, q, :], raw_of(p, k, q), HI[:, q, :].bitcast(F32),
                                        ALU.subtract).then_inc(lo_ready, 1)

            def sums(p, k):
                n, t = T * p + k.t, k.t
                if p == LAYER0:
                    deg = pacc[k.s][:, F:F + 1]
                    dve.wait_ge(lo_used, PRIME + 2 * (n + 1))
                    nc.vector.tensor_copy(column(DEG, t), deg).then_inc(deg_kept, 1)
                    nc.vector.tensor_scalar(RDEG[:, :], deg, 1.0, None, ALU.add).then_inc(deg1_kept, 1)
                    dve.wait_ge(deg1_kept, t + 1)
                    nc.vector.reciprocal(RDEG[:, :], RDEG[:, :]).then_inc(rdeg_kept, 1)
                if p == LAYER1:
                    dve.wait_ge(crossb_ready, t + 1)
                dve.wait_ge(cross_ready, n + 1)
                nc.vector.tensor_tensor(SUM[:, :], main_of(p, k.s), CROSS[:, :], ALU.add).then_inc(sum_ready, 1)
                dve.wait_ge(sum_ready, n + 1)
                if p == LAYER0:
                    dve.wait_ge(rdeg_kept, t + 1)
                    nc.vector.scalar_tensor_tensor(out=X[:, t, :], in0=SUM[:, :], scalar=RDEG[:, 0:1],
                                                   in1=X[:, t, :], op0=ALU.mult, op1=ALU.add).then_inc(y_ready, 1)
                elif p in (LAYER1, LAYER2):
                    nc.vector.scalar_tensor_tensor(out=X[:, t, :], in0=SUM[:, :], scalar=0.0, in1=X[:, t, :],
                                                   op0=ALU.max, op1=ALU.add).then_inc(y_ready, 1)
                else:
                    nc.vector.tensor_scalar(SUM2[:, :], SUM[:, :], 0.0, column(DINV, t), ALU.max,
                                            ALU.mult).then_inc(sum2_ready, 1)
                    dve.wait_ge(sum2_ready, past(p, L3) + t + 1)
                    nc.vector.tensor_tensor(Y[:, :], SUM2[:, :], R[:, t, :], ALU.add).then_inc(y_ready, 1)
                dve.wait_ge(y_ready, n + 1)
                nc.vector.memset(IDLE[:, 0:1], 0.0)
                nc.vector.bn_stats(ST[:, :], Y[:, :] if p in L3 else X[:, t, :]).then_inc(st_done, 1)
                if beyond(n):
                    dve.wait_ge(nmr_done, n)
                dve.wait_ge(st_done, n + 1)
                nc.vector.memset(IDLE[:, 1:2], 0.0)
                nc.vector.bn_aggr(MV[:, :], ST[:, :]).then_inc(mv_done, 1)

            def counted(p, k):
                if p == LAYER0:
                    dve.wait_ge(nz_used, PRIME + 2 * (k.t + 1))
                    nc.vector.tensor_copy(column(CNT, k.t), pcnt[k.s][:, 0:1]).then_inc(cnt_kept, 1)

            def scaled(p, k):
                n = T * p + k.t
                m = past(p, L3) + k.t
                if p not in L3:
                    return
                dve.wait_ge(rstd_done, n + 1)
                nc.vector.tensor_scalar(SUM2[:, :], Y[:, :], MV[:, 0:1], RSTD[:, 0:1], ALU.subtract,
                                        ALU.mult).then_inc(z_ready, 1)
                dve.wait_ge(z_ready, m + 1)
                nc.vector.tensor_tensor(SUM2[:, :], SUM2[:, :], GAIN[:, :], ALU.mult).then_inc(zg_ready, 1)
                dve.wait_ge(zg_ready, m + 1)
                if p != LAYER3C:
                    dve.wait_ge(rt_done, n)
                    if beyond(m):
                        dve.wait_ge(row_kept, m)
                    nc.vector.tensor_tensor(ROW[:, :], SUM2[:, :], SHIFT[:, :], ALU.add).then_inc(row_ready, 1)
                else:
                    nc.vector.tensor_tensor(SUM2[:, :], SUM2[:, :], SHIFT[:, :], ALU.add).then_inc(row_ready, 1)
                    dve.wait_ge(row_ready, n + 1)
                    nc.vector.tensor_tensor(X[:, k.t, :], SUM2[:, :], X[:, k.t, :], ALU.add).then_inc(out_ready, 1)

            def turned(p, k):
                if p == LAYER3C:
                    return
                dve.wait_ge(hthi_ready, T * p + k.t + 1)
                nc.vector.tensor_tensor(HTLO[:, :], pt[:, 0:F], HTHI[:, :].bitcast(F32), ALU.subtract).then_inc(
                    htlo_ready, 1)

            def dense(p, k):
                if p == LAYER0:
                    dve.wait_ge(h2hi_ready, k.t + 1)
                    nc.vector.tensor_tensor(H2LO[:, :], H2[:, :], H2HI[:, :].bitcast(F32), ALU.subtract).then_inc(
                        h2lo_ready, 1)
                if p in (LAYER2, LAYER3A, LAYER3B):
                    dve.wait_ge(dense_done, T * p + k.t + 1)
                    nc.vector.tensor_tensor((R if p == LAYER2 else HN)[:, k.t, :], pd[:, 0:F], BIAS[:, :],
                                            ALU.add).then_inc(dense_kept, 1)

            def node(p, k):
                if p == LAYER2:
                    if beyond(k.t):
                        dve.wait_ge(nt_done, k.t)
                    nc.vector.tensor_copy(NST[:, 0:K], NODE[:, k.t, :]).then_inc(nst_ready, 1)

            def cut_h(p, j):
                src = cut_source(p)
                dve.wait_ge(split_hi, cuts_before(p) + j + 1)
                if p in L3:
                    nc.vector.scalar_tensor_tensor(out=lo_of(j), in0=src[:, j, :], scalar=DINV[:, j:j + 1],
                                                   in1=hi_of(j).bitcast(F32), op0=ALU.mult,
                                                   op1=ALU.subtract).then_inc(split_lo, 1)
                else:
                    nc.vector.tensor_tensor(lo_of(j), src[:, j, :], hi_of(j).bitcast(F32), ALU.subtract).then_inc(
                        split_lo, 1)

            def cut_some(p, j0, j1):
                for j in range(j0, j1):
                    if j not in by_pool(p):
                        cut_h(p, j)

            cuts = [2]

            def weights_lo(p):
                if p in (LAYER0, LAYER2, LAYER3A, LAYER3B):
                    cuts[0] += 1
                    dve.wait_ge(w_hi, cuts[0])
                    whole, high, low = (W, WHI[:, :, :], WLO) if p == LAYER0 else (WONE, *WONE_CUT)
                    nc.vector.tensor_tensor(low[:, :, :], whole[:, :, :], high.bitcast(F32), ALU.subtract).then_inc(w_lo, 1)
                dve.wait_ge(par_in, par_count(p))

            hthi, htlo = [HTHI, H2HI], [HTLO, H2LO]

            def stats0(k):
                if isinstance(k.t, int) and k.t in (0, AHEAD):
                    dve.wait_ge(x_in[k.t // AHEAD], 16)
                nc.vector.bn_stats(ST0[:, k.s, :], X[:, k.t, :]).then_inc(st0_done, 1)

            def moments0(k):
                dve.wait_ge(st0_done, k.t + 1)
                if beyond(k.t - 1):
                    dve.wait_ge(ve0_done, k.t - 1)
                    dve.wait_ge(nm0_done, k.t - 1)
                nc.vector.memset(IDLE[:, 1:2], 0.0)
                nc.vector.bn_aggr(MV0[:, k.s, :], ST0[:, k.s, :]).then_inc(mv0_done, 1)

            def turned0(k):
                dve.wait_ge(hthi0, k.t + 1)
                if beyond(k.t - 1):
                    dve.wait_ge(dense0_done, k.t - 1)
                nc.vector.tensor_tensor(htlo[k.s][:, :], prow[k.s][:, 0:F], hthi[k.s][:, :].bitcast(F32),
                                        ALU.subtract).then_inc(htlo0, 1)

            def keep0(k):
                dve.wait_ge(h0_hi, k.t + 1)
                nc.vector.tensor_tensor(lo_of(k.t), pden[k.s][:, 0:F], hi_of(k.t).bitcast(F32), ALU.subtract).then_inc(
                    h0_lo, 1)
                dve.wait_ge(row0_ready, k.t + 1)
                nc.vector.tensor_tensor(X[:, k.t, :], pden[k.s][:, F:2 * F], X[:, k.t, :], ALU.add).then_inc(x0_added, 1)

            def step0(k):
                if k.before(T - 1):
                    turned0(k.next())
                if k.before(T - AHEAD):
                    stats0(Tile(k.u + AHEAD // 2, k.s))
                if beyond(k.t):
                    keep0(k.prev())
                if k.before(T - AHEAD):
                    moments0(Tile(k.u + AHEAD // 2, k.s))
            first = Tile(0, 0)
            for t in range(AHEAD):
                stats0(Tile(t // 2, t % 2))
                moments0(Tile(t // 2, t % 2))
            dve.wait_ge(w_hi, 1)
            nc.vector.tensor_tensor(WLO[:, :, :], W[:, :, :], WHI[:, :, :].bitcast(F32), ALU.subtract).then_inc(w_lo, 1)
            turned0(first)
            tiles(dve, step0, TAIL, 2)
            keep0(LAST)
            for q in range(2):
                positive(LAYER0, first, q)
                lo(LAYER0, first, q)
            dve.wait_ge(w_hi, 2)
            nc.vector.tensor_tensor(ENLO[:, :, :], EN[:, :, :], ENHI[:, :, :].bitcast(F32), ALU.subtract).then_inc(w_lo, 1)
            weights_lo(LAYER0)

            def general():
                dve.wait_ge(cnt_kept, T)
                nc.vector.tensor_reduce(CMAX[:, :], CNT[:, :], AX.X, ALU.max).then_inc(cmax_done, 1)
                dve.wait_ge(call_done, 1)
                nc.vector.tensor_scalar(FLAG[:, :], CALL[:, :], float(TOP), None, ALU.is_gt).then_inc(flag_done, 1)
                dve.wait_ge(flag_done, 1)
                flag = dve.value_load(FLAG[0:1, 0:1], min_val=0, max_val=1)
                with dve.If(flag):
                    dve.wait_ge(bits_set, NBITS)
                    with dve.Fori(0, T) as t:
                        dve.wait_ge(frow_in, 16 * (t + 1))
                        nc.vector.scalar_tensor_tensor(out=FTMP[:, :], in0=FROW[:, :], scalar=0.0, in1=FROW[:, :],
                                                       op0=ALU.max, op1=ALU.mult).then_inc(fsq_done, 1)
                        per = 4 * NBITS + 7
                        dve.wait_ge(fval_done, t + 1)
                        nc.vector.memset(VBITS[:, :], 0).then_inc(fbit_done, 1)
                        with dve.Fori(0, NBITS) as b:
                            done = per * t + 1 + 4 * b
                            dve.wait_ge(fbit_done, done)
                            nc.vector.tensor_tensor(CAND[:, :], VBITS[:, :], BITS[:, bass.ds(b, 1)],
                                                    ALU.bitwise_or).then_inc(fbit_done, 1)
                            dve.wait_ge(fbit_done, done + 1)
                            nc.vector.tensor_scalar(FTMP[:, :], FVAL[:, :], CAND[:, :].bitcast(F32), 0.0, ALU.is_ge,
                                                    ALU.add, accum_out=FCNT[:, :]).then_inc(fbit_done, 1)
                            dve.wait_ge(fbit_done, done + 2)
                            nc.vector.tensor_scalar(TAKE[:, :], FCNT[:, :], float(TOP), None,
                                                    ALU.is_ge).then_inc(fbit_done, 1)
                            dve.wait_ge(fbit_done, done + 3)
                            nc.vector.memset(IDLE[:, 0:1], 0.0)
                            nc.vector.copy_predicated(VBITS[:, :], TAKE[:, :], CAND[:, :]).then_inc(fbit_done, 1)
                        least = VBITS[:, :].bitcast(F32)
                        done = per * t + 1 + 4 * NBITS
                        dve.wait_ge(fbit_done, done)
                        nc.vector.tensor_scalar(FTMP[:, :], FVAL[:, :], least, 0.0, ALU.is_gt, ALU.add,
                                                accum_out=FCNT[:, :]).then_inc(fbit_done, 1)
                        dve.wait_ge(fbit_done, done + 1)
                        nc.vector.tensor_scalar(ROOM[:, :], FCNT[:, :], -1.0, float(TOP), ALU.mult,
                                                ALU.add).then_inc(fbit_done, 1)
                        dve.wait_ge(fbit_done, done + 2)
                        nc.vector.tensor_scalar(FTMP[:, :], FVAL[:, :], least, None, ALU.is_equal).then_inc(
                            fbit_done, 1)
                        dve.wait_ge(fbit_done, done + 3)
                        nc.vector.tensor_tensor_scan(FKEEP[:, :], FTMP[:, :], FTMP[:, :], 0.0, ALU.add,
                                                     ALU.max).then_inc(fbit_done, 1)
                        dve.wait_ge(fbit_done, done + 4)
                        nc.vector.scalar_tensor_tensor(out=FKEEP[:, :], in0=FKEEP[:, :], scalar=ROOM[:, :],
                                                       in1=FTMP[:, :], op0=ALU.is_le, op1=ALU.mult).then_inc(
                            fbit_done, 1)
                        dve.wait_ge(fbit_done, done + 5)
                        nc.vector.scalar_tensor_tensor(out=FKEEP[:, :], in0=FVAL[:, :], scalar=least,
                                                       in1=FKEEP[:, :], op0=ALU.is_gt, op1=ALU.add).then_inc(
                            fbit_done, 1)
                        dve.wait_ge(fbit_done, done + 6)
                        nc.vector.tensor_tensor(FROW[:, :], FROW[:, :], FKEEP[:, :], ALU.mult).then_inc(
                            fkeep_done, 1)
                    dve.wait_ge(frow_again, 64)
                dve.wait_ge(flag_done, 1)

            for p in ALL:
                early = p <= LAYER1

                def into_layer2():
                    def cut_turned(j):
                        dve.wait_ge(split_hi, T + j + 1)
                        nc.vector.tensor_tensor(lo_of(j), HN[:, j, :], hi_of(j).bitcast(F32), ALU.subtract).then_inc(
                            split_lo, 1)

                    def cut_e(i, s):
                        dve.wait_ge(ehi_ready, i + 1)
                        nc.vector.tensor_tensor(ELO[s][:, :, :], EW[:, s, :, :], EHI[s][:, :, :].bitcast(F32),
                                                ALU.subtract).then_inc(elo_ready, 1)

                    def add(i, t, k):
                        if isinstance(i, int) and i + k == 0:
                            nc.vector.tensor_scalar(ACC[:, t, :], pein[t % 4][:, 0:F], NODE[:, t, 0:1], None,
                                                    ALU.mult).then_inc(ein_added, 1)
                            return
                        nc.vector.scalar_tensor_tensor(out=ACC[:, t, :], in0=pein[t % 4][:, k * F:(k + 1) * F],
                                                       scalar=column(NODE[:, t, :], 2 * i + k), in1=ACC[:, t, :],
                                                       op0=ALU.mult, op1=ALU.add).then_inc(ein_added, 1)

                    def group(i, s, begin=False, end=False):
                        done = EIN_PRIME + i * 2 * T
                        for t in range(T):
                            if begin and FIRST_CUTS + t < T:
                                cut_turned(FIRST_CUTS + t)
                            if begin and t == 2:
                                turned(LAYER1, LAST)
                            if t == T // 3 and not end:
                                cut_e(i + 1, 1 - s)
                            if begin:
                                dve.wait_ge(dense_kept, T + t + 1)
                            dve.wait_ge(ein_done, EIN_PRIME + i * T + t + 1)
                            dve.wait_ge(ein_added, done)
                            add(i, t, 0)
                            if t:
                                dve.wait_ge(ein_added, done + max(2 * t - 2, 1))
                                add(i, t - 1, 1)
                            if end and t > 1:
                                cut_h(LAYER2, t - 2)
                        dve.wait_ge(ein_added, done + 2 * T - 2)
                        add(i, T - 1, 1)
                    prev = LAST.prev()
                    sums(LAYER1, prev)
                    for j in range(FIRST_CUTS):
                        cut_turned(j)
                    turned(LAYER1, prev)
                    cut_e(0, 0)
                    sums(LAYER1, LAST)
                    group(0, 0, begin=True)
                    weights_lo(LAYER2)
                    group(1, 1)
                    with dve.Fori(1, E_GROUPS // 2 - 1) as g:
                        group(2 * g, 0)
                        group(2 * g + 1, 1)
                    group(E_GROUPS - 2, 0)
                    node(LAYER2, first)
                    group(E_GROUPS - 1, 1, end=True)
                    dve.wait_ge(ein_done, EIN_PRIME + T * E_GROUPS)
                    lo(LAYER2, first, 0)
                    cut_some(LAYER2, T - 2, T)

                def into_layer1():
                    prev = LAST.prev()
                    sums(LAYER0, prev)
                    counted(LAYER0, LAST)
                    general()
                    squared(LAYER1, first, 0)
                    squared(LAYER1, first, 1)
                    turned(LAYER0, prev)
                    lo(LAYER1, first, 0)
                    cut_some(LAYER1, 0, HB)
                    dense(LAYER0, prev)
                    sums(LAYER0, LAST)
                    cut_some(LAYER1, HB, HB + 6)
                    turned(LAYER0, LAST)
                    cut_some(LAYER1, HB + 6, T - 1)
                    lo(LAYER1, first, 1)
                    dense(LAYER0, LAST)
                    squared(LAYER1, first.next(), 0)
                    cut_some(LAYER1, T - 1, T)
                    weights_lo(LAYER1)

                def step(k):
                    old = beyond(k.t)
                    new = k.before(T - 1)
                    if p == LAYER0 and k is LAST:
                        into_layer1()
                        return
                    if p == LAYER1 and k is LAST:
                        into_layer2()
                        return
                    if old:
                        sums(p, k.prev())
                    if p == LAYER2 or (p in L3 and old):
                        lo(p, k, 1)
                    if new:
                        squared(p, k.next(), 1)
                        positive(p, k.next(), 0)
                    if new and early:
                        lo(p, k.next(), 0)
                    if old:
                        scaled(p, k.prev())
                    if new:
                        if not early:
                            lo(p, k.next(), 0)
                        node(p, k.next())
                        positive(p, k.next(), 1)
                    if old:
                        turned(p, k.prev())
                    if k.before(T - 2):
                        squared(p, k.next().next(), 0)
                    if new and early:
                        lo(p, k.next(), 1)
                    if old:
                        dense(p, k.prev())
                    elif p in L3:
                        weights_lo(p)
                    counted(p, k)
                tiles(dve, step)
                if p <= LAYER1:
                    continue
                after = p + 1 if p + 1 in OVERLAP else None
                if after:
                    lo(after, first, 0)
                    cut_some(after, 0, HB)
                sums(p, LAST)
                if after:
                    cut_some(after, HB, HB + 6)
                scaled(p, LAST)
                if after:
                    cut_some(after, HB + 6, T - 4)
                turned(p, LAST)
                if after:
                    cut_some(after, T - 4, T - 1)
                    lo(after, first, 1)
                dense(p, LAST)
                if after:
                    cut_some(after, T - 1, T)

        @block.tensor
        def _(pe):
            def cut_product(psum, lhs, rhs):
                for a in range(C):
                    for i, (l, r) in enumerate(((0, 0), (0, 1), (1, 0))):
                        mm = nc.tensor.matmul(psum, lhs(l, a), rhs(r, a), start=a == 0 and i == 0,
                                              stop=a == C - 1 and i == 2)
                return mm

            def part(p, k, q, low, between={}, blocks=(0, HB)):
                n = 2 * T * p + 2 * k.t + q
                s = k.s
                end = q == 1

                def cut_is_there(j):
                    if p and isinstance(k.t, int) and k.t == 0:
                        pe.wait_ge(*low_parts(p, q * HB + j))
                if not low:
                    pe.wait_ge(hi_ready, n + 1)
                    for j in range(*blocks):
                        if j in between:
                            between[j]()
                        lhs = HI[:, q, j * P:(j + 1) * P]
                        b = q * HB + j
                        cut_is_there(j)
                        begin = q == 0 and j == 0
                        if p == LAYER0:
                            nc.tensor.matmul(pacc[s][:, 0:F + 2], lhs, H[:, b, 0:F + 2], start=begin,
                                             stop=end and j == HB - 1)
                            mm = nc.tensor.matmul(pcross[s][:, 0:F], lhs, lo_of(b), start=begin,
                                                  stop=end and j == HB - 1)
                        else:
                            both = bass.AP(H, b * HC, [[T * HC, P], [F + ONE, 2], [1, F]])
                            mm = nc.tensor.matmul(pacc[s][:, :], lhs, both, start=begin, stop=end and j == HB - 1)
                    if blocks[1] == HB:
                        mm.then_inc(hi_used, 1)
                else:
                    w = F + 2 if p == LAYER0 else F
                    pe.wait_ge(lo_ready, RAW_PRIME + n + 1)
                    for j in range(*blocks):
                        mm = nc.tensor.matmul(pacc[s][:, 0:w], LO[:, q, j * P:(j + 1) * P], H[:, q * HB + j, 0:w],
                                              start=False, stop=False, skip_group_check=True)
                    if blocks[1] == HB:
                        mm.then_inc(lo_used, 1)

            def count(p, k):
                if p == LAYER0:
                    for q in range(2):
                        pe.wait_ge(nz_ready, 2 * k.t + q + 1)
                        for j in range(HB):
                            mm = nc.tensor.matmul(pcnt[k.s][:, 0:2], NZ[:, q, j * P:(j + 1) * P], ONEB[:, :],
                                                  start=q == 0 and j == 0, stop=q == 1 and j == HB - 1)
                        mm.then_inc(nz_used, 1)

            TURN_AT, DENSE_AT = 6, 11

            def turn(p, k):
                n = T * p + k.t
                if p == LAYER3C:
                    return
                pe.wait_ge(row_ready, n + 1)
                if beyond(n):
                    pe.wait_ge(htlo_ready, n)
                for a in range(C):
                    mm = nc.tensor.transpose(pt[:, a * P:(a + 1) * P], ROW[:, a * P:(a + 1) * P], IDN[:, :])
                mm.then_inc(rt_done, 1)

            cuts_of = {LAYER0: 3, LAYER1: 3, LAYER2: 4, LAYER3A: 5, LAYER3B: 6}
            w = (WHI, WLO)
            ht = (HTHI, HTLO)
            h2 = (H2HI, H2LO)

            def dense_a(p, k):
                n = T * p + k.t
                if p == LAYER3C:
                    return
                pe.wait_ge(htlo_ready, n + 1)
                pe.wait_ge(w_lo, cuts_of[p])
                if beyond(n):
                    pe.wait_ge(dense_kept, n)
                if p == LAYER0:
                    for b in range(C):
                        mm = cut_product(pd[:, b * P:(b + 1) * P], lambda l, a: w[l][:, a, b * P:(b + 1) * P],
                                         lambda r, a: ht[r][:, a * P:(a + 1) * P])
                    mm.then_inc(proj_done, 1)
                elif p == LAYER1:
                    cut_product(pd[:, 0:K], lambda l, a: ht[l][:, a * P:(a + 1) * P],
                                lambda r, a: (ENHI, ENLO)[r][:, a, :]).then_inc(dense_done, 1)
                else:
                    cut_product(pd[:, 0:F], lambda l, a: ht[l][:, a * P:(a + 1) * P],
                                lambda r, a: WONE_CUT[r][:, a, :]).then_inc(dense_done, 1)

            def dense_b(p, k):
                if p == LAYER0:
                    pe.wait_ge(h2lo_ready, k.t + 1)
                    cut_product(pd[:, F:2 * F], lambda l, a: h2[l][:, a * P:(a + 1) * P],
                                lambda r, a: w[r][:, a, F:2 * F]).then_inc(dense_done, 1)

            pe.wait_ge(w0_in, 48)
            for f in range(C):
                for a in range(C):
                    mm = nc.tensor.matmul(pd[:, f * F:(f + 1) * F], R[:, T - 4 + a, f * P:(f + 1) * P],
                                          R[:, T - 2 + a, :],
                                          start=a == 0, stop=a == C - 1)
            mm.then_inc(wc_done, 1)

            rows, hthi, htlo = [ROW, Y], [HTHI, H2HI], [HTLO, H2LO]

            def turn0(k):
                pe.wait_ge(row0_ready, k.t + 1)
                if beyond(k.t - 1):
                    pe.wait_ge(htlo0, k.t - 1)
                for a in range(C):
                    mm = nc.tensor.transpose(prow[k.s][:, a * P:(a + 1) * P], rows[k.s][:, a * P:(a + 1) * P],
                                             IDN[:, :])
                mm.then_inc(rt0_done, 1)

            def step0(k):
                if k.before(T - 2):
                    turn0(k.next().next())
                pe.wait_ge(htlo0, k.t + 1)
                if beyond(k.t - 1):
                    pe.wait_ge(h0_lo, k.t - 1)
                    pe.wait_ge(x0_added, k.t - 1)
                cut = (hthi[k.s], htlo[k.s])
                cut_product(pden[k.s][:, :], lambda l, a: cut[l][:, a * P:(a + 1) * P],
                            lambda r, a: w[r][:, a, :]).then_inc(dense0_done, 1)
            pe.wait_ge(ident_set, 4)
            turn0(Tile(0, 0))
            turn0(Tile(0, 1))
            pe.wait_ge(w_lo, 1)
            tiles(pe, step0, TAIL, 2)
            pe.wait_ge(h0_lo, T)
            pe.wait_ge(x0_added, T)
            pe.wait_ge(ones_set, 2)
            pe.wait_ge(const_in, 48)

            def general():
                pe.wait_ge(flag_done, 1)
                flag = pe.value_load(FLAG[0:1, 0:1], min_val=0, max_val=1)
                with pe.If(flag):
                    with pe.Fori(0, T) as t:
                        pe.wait_ge(fkeep_done, t + 1)
                        for b in range(FBLOCKS):
                            if b >= 2:
                                pe.wait_ge(fout_ready, FBLOCKS * t + b - 1)
                            for c in range(4 * b, min(4 * b + 4, T)):
                                mm = nc.tensor.transpose(pturn[b % 2][:, (c % 4) * P:(c % 4 + 1) * P],
                                                         FROW[:, c * P:(c + 1) * P], IDN[:, :])
                            mm.then_inc(fturned, 1)
                pe.wait_ge(flag_done, 1)

            for p in ALL:
                if p == LAYER2:
                    def group(i, s, between={}):
                        pe.wait_ge(elo_ready, i + 1)
                        for t in range(T):
                            if t in between:
                                between[t]()
                            last = t - 4 if t >= 4 else max(v for v in range(T) if v % 4 == t)
                            done = EIN_PRIME + (i - (t < 4)) * 2 * T
                            pe.wait_ge(split_lo, T + t + 1 - len(by_pool(LAYER1)))
                            pe.wait_ge(ein_added, done + min(2 * last + 3, 2 * T))
                            left = (H[:, t, 0:F], lo_of(t))
                            cut_product(pein[t % 4][:, :], lambda l, a: left[l][:, a * P:(a + 1) * P],
                                        lambda r, a: (EHI, ELO)[r][s][:, a, :]).then_inc(ein_done, 1)
                    group(0, 0, {3: lambda: turn(LAYER1, LAST), 5: lambda: dense_a(LAYER1, LAST)})
                    group(1, 1)
                    with pe.Fori(1, E_GROUPS // 2) as g:
                        group(2 * g, 0)
                        group(2 * g + 1, 1)

                def step(k):
                    n = T * p + k.t
                    if p == LAYER2:
                        if not beyond(k.t):
                            v = T - 1 - (T - 3) % 4
                            pe.wait_ge(ein_added, EIN_PRIME + 2 * T * (E_GROUPS - 1) + min(2 * v + 3, 2 * T))
                        pe.wait_ge(nst_ready, k.t + 1)
                        if beyond(k.t):
                            pe.wait_ge(ntt_ready, k.t)
                        nc.tensor.transpose(pnode[:, 0:P], NST[:, :], IDN[:, :]).then_inc(nt_done, 1)
                    if beyond(n - 1):
                        pe.wait_ge(sum_ready, n - 1)
                        if p == LAYER0:
                            pe.wait_ge(cnt_kept, k.t - 1)
                    part(p, k, 0, False)
                    part(p, k, 0, True)
                    count(p, k)
                    if beyond(k.t - 1):
                        dense_b(p, k.prev().prev())
                    if p in OVERLAP and not beyond(k.t):
                        if p == LAYER1:
                            dense_b(LAYER0, LAST.prev())
                        most = (0, HB - 1)
                        part(p, k, 1, False, {TURN_AT: lambda: turn(p - 1, LAST),
                                              DENSE_AT: lambda: dense_a(p - 1, LAST)}, most)
                        part(p, k, 1, True, blocks=most)
                        if p == LAYER1:
                            dense_b(LAYER0, LAST)
                        part(p, k, 1, False, blocks=(HB - 1, HB))
                        part(p, k, 1, True, blocks=(HB - 1, HB))
                        return
                    part(p, k, 1, False)
                    into_layer1 = p == LAYER0 and k is LAST
                    if beyond(k.t) and not into_layer1:
                        turn(p, k.prev())
                    if p == LAYER2:
                        pe.wait_ge(ntt_ready, k.t + 1)
                        nc.tensor.matmul(pacc[k.s][:, 0:F], NTT[:, :], NB[:, :], start=False, stop=False,
                                         skip_group_check=True)
                    part(p, k, 1, True)
                    if into_layer1:
                        general()
                        turn(p, k.prev())
                        dense_a(p, k.prev())
                    elif beyond(k.t):
                        dense_a(p, k.prev())
                tiles(pe, step)


def kernel(**inputs):
    import numpy as np
    import concourse.bacc as bacc
    from concourse.bass_utils import run_bass_kernel_spmd

    a = {k: np.asarray(v) for k, v in inputs.items()}
    x = np.zeros((NP, F), np.float32)
    x[:N] = a["x"]
    adj = np.zeros((NP, NP), np.float32)
    adj[:N, :N] = a["adj"]
    arrays = {
        "x": x.reshape(T, P, F).transpose(1, 0, 2).reshape(P, T * F),
        "adjn": adj.reshape(T, P, NP),
        "adjb": adj.reshape(T, P, T, P).transpose(0, 3, 2, 1).reshape(T, P, NP),
        "neigh_w": a["L0_gnn_neigh_W"],
        "lin_wt": a["L0_gnn_lin_W"].T,
        "w_proj": a["L1_gnn_W_proj"], "b_proj": a["L1_gnn_b_proj"].reshape(C, P).T,
        "w_gcn": a["L1_gnn_W_gcn"], "b_gcn": a["L1_gnn_b_gcn"],
        "e_w1": a["L2_gnn_W1"],
        "e_w2": a["L2_gnn_W2"].reshape(K // 2, 2, C, P, F).transpose(0, 3, 2, 1, 4).reshape(K // 2, P, C, 2 * F),
        "e_b": a["L2_gnn_b"],
        "w1": a["L3_gnn_W1"], "b1": a["L3_gnn_b1"], "w2": a["L3_gnn_W2"], "b2": a["L3_gnn_b2"],
        "w3": a["L3_gnn_W3"], "b3": a["L3_gnn_b3"],
        "g1": a["L3_gnn_g1"], "be1": a["L3_gnn_be1"], "g2": a["L3_gnn_g2"], "be2": a["L3_gnn_be2"],
        "g3": a["L3_gnn_g3"], "be3": a["L3_gnn_be3"],
    }
    nc = bacc.Bacc("TRN2", target_bir_lowering=False, num_devices=1)
    feed, args = {}, {}
    for name, array in arrays.items():
        array = np.ascontiguousarray(array)
        feed[f"in_{name}"] = array
        args[name] = nc.dram_tensor(f"in_{name}", array.shape, mybir.dt.from_np(array.dtype), kind="ExternalInput").ap()
    out = nc.dram_tensor("out", (T, P, F), F32, kind="ExternalOutput").ap()
    adjf = nc.dram_tensor("adj_top", (T, P, NP), F32, kind="Internal").ap()
    build(nc, out=out, adjf=adjf, **args)
    r = run_bass_kernel_spmd(nc, [feed], core_ids=[0])
    return r.results[0]["out"].reshape(NP, F)[:N]
```
